# Optimizing a Trainium2 kernel written in Bass

```python
import numpy as np
import jax
import jax.numpy as jnp

def _softmax(x, axis=-1):
    return jax.nn.softmax(x, axis=axis)

def _gelu(x):
    return jax.nn.gelu(x, approximate=True)

def _silu(x):
    return jax.nn.silu(x)

def _sigmoid(x):
    return jax.nn.sigmoid(x)

def _layernorm(x, axis=-1, eps=1e-05):
    m = jnp.mean(x, axis=axis, keepdims=True)
    v = jnp.var(x, axis=axis, keepdims=True)
    return (x - m) / jnp.sqrt(v + eps)

def _scatter_add(tgt, idx, src, axis=0):
    return tgt.at[idx].add(src)

def _segment_sum(src, seg, n):
    return jax.ops.segment_sum(src, seg, n)
kernel_name = 'mk_gnn_preln_d4_gnn_r8_854335'

def setup_inputs(seed: int=0):
    np.random.seed(seed)
    _w = jnp.asarray

    def _rec_inputs():
        import jax
        import jax.numpy as jnp
        _gk = jax.random.key(seed)
        x = -0.0005121 + 1.001 * jax.random.normal(jax.random.fold_in(_gk, 1), (12500, 64), jnp.float32)
        src = jax.random.randint(jax.random.fold_in(_gk, 2), (200000,), 0, 12500, jnp.int32)
        dst = jnp.minimum((12500 * jax.random.uniform(jax.random.fold_in(_gk, 3), (200000,)) ** 2.0).astype(jnp.int32), 99999)
        _o = jnp.argsort(dst, stable=True)
        src = src[_o]
        dst = dst[_o]
        edge_attr_64 = -6.74381e-05 + 0.999835 * jax.random.normal(jax.random.fold_in(_gk, 12), (200000, 64), jnp.float32)
        edge_weight = jax.random.uniform(jax.random.fold_in(_gk, 14), (200000,), jnp.float32, 0.0, 0.999999)
        return (x, src, dst, edge_attr_64, edge_weight)
    x, src, dst, edge_attr_64, edge_weight = _rec_inputs()

    def _L0_gnn_setup():
        import jax, jax.numpy as jnp
        import numpy as np
        V, E, D = (6250, 156250, 64)
        LOG2 = float(np.log(2.0))

        def ssp(x):
            return jax.nn.softplus(x) - LOG2
        key = jax.random.key(seed)
        ks = jax.random.split(key, 10)
        s = 1.0 / np.sqrt(D)
        return {'node_feats': jax.random.normal(ks[0], (V, D), jnp.float32), 'edge_feats': jax.random.normal(ks[1], (E, D), jnp.float32), 'src': jax.random.randint(ks[2], (E,), 0, V, jnp.int32), 'dst': jax.random.randint(ks[3], (E,), 0, V, jnp.int32), 'We1': jax.random.normal(ks[4], (D, D), jnp.float32) * s, 'be1': jnp.zeros((D,), jnp.float32), 'We2': jax.random.normal(ks[5], (D, D), jnp.float32) * s, 'be2': jnp.zeros((D,), jnp.float32), 'Wn': jax.random.normal(ks[6], (D, D), jnp.float32) * s, 'bn': jnp.zeros((D,), jnp.float32), 'Wc': jax.random.normal(ks[7], (D, D), jnp.float32) * s, 'bc': jnp.zeros((D,), jnp.float32), 'Wo': jax.random.normal(ks[8], (D, D), jnp.float32) * s, 'bo': jnp.zeros((D,), jnp.float32)}
    _L0_gnn_all = _L0_gnn_setup()
    _L0_gnn_in = {k: v for k, v in _L0_gnn_all.items() if k in ('We1', 'be1', 'We2', 'be2', 'Wn', 'bn', 'Wc', 'bc', 'Wo', 'bo')}
    del _L0_gnn_all

    def _L1_gnn_setup():
        import jax, jax.numpy as jnp
        import numpy as np
        N_NODES = 12500
        N_EDGES = 200000
        IN_DIM = 64
        OUT_DIM = 64
        BN_EPS = 1e-05

        def batchnorm(h, gamma, beta):
            mean = jnp.mean(h, axis=0)
            var = jnp.mean((h - mean) ** 2, axis=0)
            return gamma * (h - mean) * jax.lax.rsqrt(var + BN_EPS) + beta
        key = jax.random.key(seed)
        ks = jax.random.split(key, 4)
        x = jax.random.normal(ks[0], (N_NODES, IN_DIM), dtype=jnp.float32)
        edge_index = jax.random.randint(ks[1], (2, N_EDGES), 0, N_NODES, dtype=jnp.int32)
        epsilon = jnp.asarray(0.1, dtype=jnp.float32)
        W1 = jax.random.normal(ks[2], (IN_DIM, 2 * OUT_DIM), dtype=jnp.float32) * (1.0 / np.sqrt(IN_DIM))
        b1 = jnp.zeros((2 * OUT_DIM,), dtype=jnp.float32)
        g1 = jnp.ones((2 * OUT_DIM,), dtype=jnp.float32)
        be1 = jnp.zeros((2 * OUT_DIM,), dtype=jnp.float32)
        W2 = jax.random.normal(ks[3], (2 * OUT_DIM, OUT_DIM), dtype=jnp.float32) * (1.0 / np.sqrt(2 * OUT_DIM))
        b2 = jnp.zeros((OUT_DIM,), dtype=jnp.float32)
        g2 = jnp.ones((OUT_DIM,), dtype=jnp.float32)
        be2 = jnp.zeros((OUT_DIM,), dtype=jnp.float32)
        return {'x': x, 'edge_index': edge_index, 'epsilon': epsilon, 'W1': W1, 'b1': b1, 'g1': g1, 'be1': be1, 'W2': W2, 'b2': b2, 'g2': g2, 'be2': be2}
    _L1_gnn_all = _L1_gnn_setup()
    _L1_gnn_in = {k: v for k, v in _L1_gnn_all.items() if k in ('epsilon', 'W1', 'b1', 'g1', 'be1', 'W2', 'b2', 'g2', 'be2')}
    del _L1_gnn_all

    def _L2_gnn_setup():
        import jax, jax.numpy as jnp
        import numpy as np
        N_NODES = 12500
        N_EDGES = 200000
        D_IN = 64
        D_OUT = 64
        LEAKY_SLOPE = 0.01
        key = jax.random.key(seed)
        k1, k2, k3, k4, k5 = jax.random.split(key, 5)
        feat = jax.random.normal(k1, (N_NODES, D_IN), dtype=jnp.float32)
        scale = jnp.sqrt(2.0 / (D_IN + D_OUT)).astype(jnp.float32)
        W1 = jax.random.normal(k2, (D_IN, D_OUT), dtype=jnp.float32) * scale
        W2 = jax.random.normal(k3, (D_IN, D_OUT), dtype=jnp.float32) * scale
        src = jax.random.randint(k4, (N_EDGES,), 0, N_NODES, dtype=jnp.int64 if jax.config.jax_enable_x64 else jnp.int32)
        dst = jax.random.randint(k5, (N_EDGES,), 0, N_NODES, dtype=jnp.int64 if jax.config.jax_enable_x64 else jnp.int32)
        return {'feat': feat, 'W1': W1, 'W2': W2, 'src': src, 'dst': dst}
    _L2_gnn_all = _L2_gnn_setup()
    _L2_gnn_in = {k: v for k, v in _L2_gnn_all.items() if k in ('W1', 'W2')}
    del _L2_gnn_all

    def _L3_gnn_setup():
        import jax, jax.numpy as jnp
        import numpy as np
        BN_EPS = 0.001
        N_NODES, D_IN, D_HID, N_EDGES = (12500, 64, 64, 200000)

        def _bn_relu(x, gamma, beta, mean, var):
            return jax.nn.relu((x - mean) * jax.lax.rsqrt(var + BN_EPS) * gamma + beta)
        key = jax.random.key(seed)
        ks = jax.random.split(key, 8)
        node_repr = jax.random.normal(ks[0], (N_NODES, D_IN), dtype=jnp.float32)
        edges = jax.random.randint(ks[1], (2, N_EDGES), 0, N_NODES, dtype=jnp.int32)
        edge_weights = jax.random.uniform(ks[2], (N_EDGES,), dtype=jnp.float32)
        W_prep = jax.random.normal(ks[3], (D_IN, D_HID), dtype=jnp.float32) * np.sqrt(2.0 / D_IN)
        b_prep = jnp.zeros((D_HID,), jnp.float32)
        gamma_p = jnp.ones((D_HID,), jnp.float32)
        beta_p = jnp.zeros((D_HID,), jnp.float32)
        mean_p = jnp.zeros((D_HID,), jnp.float32)
        var_p = jnp.ones((D_HID,), jnp.float32)
        W_upd = jax.random.normal(ks[4], (D_IN + D_HID, D_HID), dtype=jnp.float32) * np.sqrt(2.0 / (D_IN + D_HID))
        b_upd = jnp.zeros((D_HID,), jnp.float32)
        gamma_u = jnp.ones((D_HID,), jnp.float32)
        beta_u = jnp.zeros((D_HID,), jnp.float32)
        mean_u = jnp.zeros((D_HID,), jnp.float32)
        var_u = jnp.ones((D_HID,), jnp.float32)
        return dict(node_repr=node_repr, edges=edges, edge_weights=edge_weights, W_prep=W_prep, b_prep=b_prep, gamma_p=gamma_p, beta_p=beta_p, mean_p=mean_p, var_p=var_p, W_upd=W_upd, b_upd=b_upd, gamma_u=gamma_u, beta_u=beta_u, mean_u=mean_u, var_u=var_u)
    _L3_gnn_all = _L3_gnn_setup()
    _L3_gnn_in = {k: v for k, v in _L3_gnn_all.items() if k in ('W_prep', 'b_prep', 'gamma_p', 'beta_p', 'mean_p', 'var_p', 'W_upd', 'b_upd', 'gamma_u', 'beta_u', 'mean_u', 'var_u')}
    del _L3_gnn_all
    return {'x': x, 'src': src, 'dst': dst, 'edge_attr_64': edge_attr_64, 'edge_weight': edge_weight, 'L0_gnn_We1': _L0_gnn_in['We1'], 'L0_gnn_be1': _L0_gnn_in['be1'], 'L0_gnn_We2': _L0_gnn_in['We2'], 'L0_gnn_be2': _L0_gnn_in['be2'], 'L0_gnn_Wn': _L0_gnn_in['Wn'], 'L0_gnn_bn': _L0_gnn_in['bn'], 'L0_gnn_Wc': _L0_gnn_in['Wc'], 'L0_gnn_bc': _L0_gnn_in['bc'], 'L0_gnn_Wo': _L0_gnn_in['Wo'], 'L0_gnn_bo': _L0_gnn_in['bo'], 'L1_gnn_epsilon': _L1_gnn_in['epsilon'], 'L1_gnn_W1': _L1_gnn_in['W1'], 'L1_gnn_b1': _L1_gnn_in['b1'], 'L1_gnn_g1': _L1_gnn_in['g1'], 'L1_gnn_be1': _L1_gnn_in['be1'], 'L1_gnn_W2': _L1_gnn_in['W2'], 'L1_gnn_b2': _L1_gnn_in['b2'], 'L1_gnn_g2': _L1_gnn_in['g2'], 'L1_gnn_be2': _L1_gnn_in['be2'], 'L2_gnn_W1': _L2_gnn_in['W1'], 'L2_gnn_W2': _L2_gnn_in['W2'], 'L3_gnn_W_prep': _L3_gnn_in['W_prep'], 'L3_gnn_b_prep': _L3_gnn_in['b_prep'], 'L3_gnn_gamma_p': _L3_gnn_in['gamma_p'], 'L3_gnn_beta_p': _L3_gnn_in['beta_p'], 'L3_gnn_mean_p': _L3_gnn_in['mean_p'], 'L3_gnn_var_p': _L3_gnn_in['var_p'], 'L3_gnn_W_upd': _L3_gnn_in['W_upd'], 'L3_gnn_b_upd': _L3_gnn_in['b_upd'], 'L3_gnn_gamma_u': _L3_gnn_in['gamma_u'], 'L3_gnn_beta_u': _L3_gnn_in['beta_u'], 'L3_gnn_mean_u': _L3_gnn_in['mean_u'], 'L3_gnn_var_u': _L3_gnn_in['var_u']}

def reference(x, src, dst, edge_attr_64, edge_weight, L0_gnn_We1, L0_gnn_be1, L0_gnn_We2, L0_gnn_be2, L0_gnn_Wn, L0_gnn_bn, L0_gnn_Wc, L0_gnn_bc, L0_gnn_Wo, L0_gnn_bo, L1_gnn_epsilon, L1_gnn_W1, L1_gnn_b1, L1_gnn_g1, L1_gnn_be1, L1_gnn_W2, L1_gnn_b2, L1_gnn_g2, L1_gnn_be2, L2_gnn_W1, L2_gnn_W2, L3_gnn_W_prep, L3_gnn_b_prep, L3_gnn_gamma_p, L3_gnn_beta_p, L3_gnn_mean_p, L3_gnn_var_p, L3_gnn_W_upd, L3_gnn_b_upd, L3_gnn_gamma_u, L3_gnn_beta_u, L3_gnn_mean_u, L3_gnn_var_u):
    import jax
    import jax.numpy as jnp

    def _L0_gnn_ref(node_feats, edge_feats, src, dst, We1, be1, We2, be2, Wn, bn, Wc, bc, Wo, bo):
        import jax, jax.numpy as jnp
        import numpy as np
        V, E, D = (6250, 156250, 64)
        LOG2 = float(np.log(2.0))

        def ssp(x):
            return jax.nn.softplus(x) - LOG2
        f = ssp(edge_feats @ We1 + be1)
        f = ssp(f @ We2 + be2)
        h = node_feats @ Wn + bn
        msg = h[src] * f
        agg = jax.ops.segment_sum(msg, dst, num_segments=node_feats.shape[0])
        out = ssp(agg @ Wc + bc)
        return out @ Wo + bo

    def _L1_gnn_ref(x, edge_index, epsilon, W1, b1, g1, be1, W2, b2, g2, be2):
        import jax, jax.numpy as jnp
        import numpy as np
        N_NODES = 12500
        N_EDGES = 200000
        IN_DIM = 64
        OUT_DIM = 64
        BN_EPS = 1e-05

        def batchnorm(h, gamma, beta):
            mean = jnp.mean(h, axis=0)
            var = jnp.mean((h - mean) ** 2, axis=0)
            return gamma * (h - mean) * jax.lax.rsqrt(var + BN_EPS) + beta
        src, dst = (edge_index[0], edge_index[1])
        neighbor_sum = jnp.zeros_like(x).at[dst].add(x[src])
        combined = (1.0 + epsilon) * x + neighbor_sum
        h = combined @ W1 + b1
        h = jax.nn.relu(batchnorm(h, g1, be1))
        h = h @ W2 + b2
        return batchnorm(h, g2, be2)

    def _L2_gnn_ref(feat, W1, W2, src, dst):
        import jax, jax.numpy as jnp
        import numpy as np
        N_NODES = 12500
        N_EDGES = 200000
        D_IN = 64
        D_OUT = 64
        LEAKY_SLOPE = 0.01
        N = feat.shape[0]
        ones = jnp.ones(src.shape[0], dtype=feat.dtype)
        deg = jnp.maximum(jax.ops.segment_sum(ones, src, num_segments=N), 1.0)
        self_term = feat @ W1
        inter = self_term[src] + feat[src] * feat[dst] @ W2
        norm = jnp.sqrt(deg[src] * deg[dst])[:, None]
        msg = inter / norm
        agg = jax.ops.segment_sum(msg, dst, num_segments=N)
        embed = self_term + agg
        return jax.nn.leaky_relu(embed, negative_slope=LEAKY_SLOPE)

    def _L3_gnn_ref(node_repr, edges, edge_weights, W_prep, b_prep, gamma_p, beta_p, mean_p, var_p, W_upd, b_upd, gamma_u, beta_u, mean_u, var_u):
        import jax, jax.numpy as jnp
        import numpy as np
        BN_EPS = 0.001
        N_NODES, D_IN, D_HID, N_EDGES = (12500, 64, 64, 200000)

        def _bn_relu(x, gamma, beta, mean, var):
            return jax.nn.relu((x - mean) * jax.lax.rsqrt(var + BN_EPS) * gamma + beta)
        num_nodes = node_repr.shape[0]
        dst, src = (edges[0], edges[1])
        nbr = node_repr[src]
        msgs = _bn_relu(nbr @ W_prep + b_prep, gamma_p, beta_p, mean_p, var_p)
        msgs = msgs * edge_weights[:, None]
        agg = jax.ops.segment_sum(msgs, dst, num_segments=num_nodes)
        cnt = jax.ops.segment_sum(jnp.ones_like(edge_weights), dst, num_segments=num_nodes)
        agg = agg / jnp.maximum(cnt, 1.0)[:, None]
        h = jnp.concatenate([node_repr, agg], axis=1)
        return _bn_relu(h @ W_upd + b_upd, gamma_u, beta_u, mean_u, var_u)
    edge_index = jnp.stack([src, dst])
    h = jnp.maximum(_layernorm(x, axis=-1), 0.0)
    x = x + _L0_gnn_ref(h, edge_attr_64, src, dst, L0_gnn_We1, L0_gnn_be1, L0_gnn_We2, L0_gnn_be2, L0_gnn_Wn, L0_gnn_bn, L0_gnn_Wc, L0_gnn_bc, L0_gnn_Wo, L0_gnn_bo)
    h = jnp.maximum(_layernorm(x, axis=-1), 0.0)
    x = x + _L1_gnn_ref(h, edge_index, L1_gnn_epsilon, L1_gnn_W1, L1_gnn_b1, L1_gnn_g1, L1_gnn_be1, L1_gnn_W2, L1_gnn_b2, L1_gnn_g2, L1_gnn_be2)
    h = jnp.maximum(_layernorm(x, axis=-1), 0.0)
    x = x + _L2_gnn_ref(h, L2_gnn_W1, L2_gnn_W2, src, dst)
    h = jnp.maximum(_layernorm(x, axis=-1), 0.0)
    x = x + _L3_gnn_ref(h, edge_index, edge_weight, L3_gnn_W_prep, L3_gnn_b_prep, L3_gnn_gamma_p, L3_gnn_beta_p, L3_gnn_mean_p, L3_gnn_var_p, L3_gnn_W_upd, L3_gnn_b_upd, L3_gnn_gamma_u, L3_gnn_beta_u, L3_gnn_mean_u, L3_gnn_var_u)
    return x

_drawn_inputs = setup_inputs


def setup_inputs(seed=0):
    import zlib

    import numpy as np

    out = dict(_drawn_inputs(seed))
    spreads = {'L0_gnn_be1': (0.0, 0.1),
     'L0_gnn_be2': (0.0, 0.1),
     'L0_gnn_bn': (0.0, 0.1),
     'L0_gnn_bc': (0.0, 0.1),
     'L0_gnn_bo': (0.0, 0.1),
     'L1_gnn_b1': (0.0, 2.0),
     'L1_gnn_g1': (1.0, 0.2),
     'L1_gnn_be1': (0.0, 0.1),
     'L1_gnn_b2': (0.0, 2.0),
     'L1_gnn_g2': (1.0, 0.2),
     'L1_gnn_be2': (0.0, 0.1),
     'L3_gnn_b_prep': (0.0, 0.593),
     'L3_gnn_gamma_p': (1.0, 0.6),
     'L3_gnn_beta_p': (0.0, 0.677),
     'L3_gnn_mean_p': (0.0, 0.556),
     'L3_gnn_var_p': (1.0, 0.6),
     'L3_gnn_b_upd': (0.0, 0.275),
     'L3_gnn_gamma_u': (1.0, 0.2),
     'L3_gnn_beta_u': (0.0, 0.283),
     'L3_gnn_mean_u': (0.0, 0.302),
     'L3_gnn_var_u': (1.0, 0.2)}
    factors = {'edge_weight': 2.873}
    for name, (base, spread) in spreads.items():
        noise = np.random.default_rng([zlib.crc32(name.encode()), seed]).standard_normal(out[name].shape)
        drawn = base * np.exp(spread * noise) if base else spread * noise
        out[name] = jnp.asarray(drawn.astype(out[name].dtype))
    for name, factor in factors.items():
        out[name] = (out[name] * factor).astype(out[name].dtype)
    return out
```

```python
import concourse.bass as bass
from concourse import mybir
from contextlib import ExitStack

FP32 = mybir.dt.float32
BF16 = mybir.dt.bfloat16
I32 = mybir.dt.int32
ALU = mybir.AluOpType
ACT = mybir.ActivationFunctionType
AX = mybir.AxisListType

D = 64
P = 128
P_NODE = 125
TILES = 4
STEP = TILES * P
SLOTS = 3
WINDOW = 128
CB = 4
CN = CB * P_NODE
CF = CB * D
LOG2 = 0.6931471805599453
CLAMP = 30.0
LN_EPS = 1e-5
BN1_EPS = 1e-5
BN3_EPS = 1e-3
LEAKY = 0.01
SPARE = CN


class Item:

    def __init__(self, rnd, off, unroll):
        self.slot = off % unroll
        self.round = rnd + off // unroll
        self.n = rnd * unroll + off


def turns(eng, count, unroll, lead, lag, body, peel=0):

    def fixed(t):
        return lambda o: Item(0, t + o, unroll) if 0 <= t + o < count else None

    first = max(-(-lag // unroll), peel)
    last = (count - lead) // unroll
    if last - first < 1:
        for t in range(-lead, count + lag):
            body(fixed(t))
        return
    for t in range(-lead, first * unroll):
        body(fixed(t))
    with eng.Fori(first, last) as rnd:
        for s in range(unroll):
            body(lambda o, s=s: Item(rnd, s + o, unroll))
    for t in range(last * unroll, count + lag):
        body(fixed(t))


def gnn_layers(nc, io, table, acc):
    N = io["x"].shape[0]
    E = io["src"].shape[0]
    BLOCKS = N // P_NODE
    NC = BLOCKS // CB
    G = -(-E // STEP)
    TAIL = E - (G - 1) * STEP
    NW = -(-N // WINDOW)
    GR = -(-G // P)
    assert N % CN == 0 and G % SLOTS == 1 and TAIL % TILES == 0 and G <= 512 and BLOCKS <= 512 and G > SLOTS

    ctx = ExitStack()
    with ctx:
        def sb(name, shape, dt=FP32):
            return ctx.enter_context(nc.sbuf_tensor(name, shape, dt))

        def bank(name, shape, dt=FP32):
            return ctx.enter_context(nc.psum_tensor(name, shape, dt))

        def sem(name):
            return ctx.enter_context(nc.semaphore(name))

        ZF = 4 * D
        x_nm = sb("x_nm", [P_NODE, BLOCKS * D])
        aggT = sb("aggT", [P, max(N + WINDOW, GR * 3 * STEP, 12 * TILES * P)])
        SHARED = 6 * SLOTS * TILES * D
        hT = sb("hT", [P, max(N, SHARED, GR * 3 * STEP)])
        src_f = sb("src_f", [P, G * TILES])
        dst_rel = sb("dst_rel", [P, G * TILES])
        w_edge = sb("w_edge", [P, G * TILES])
        node_pb = sb("node_pb", [P, 2 * G * TILES], BF16)
        node_p, node_b = node_pb[:, 0:G * TILES], node_pb[:, G * TILES:2 * G * TILES]
        to_spare = node_pb[:, :].bitcast(FP32)
        dst_f = sb("dst_f", [P, G * TILES])
        base_i = sb("base_i", [1, G], I32)
        upper = sb("upper", [P, P])
        ones_pp = sb("ones_pp", [P, P])
        zeros = sb("zeros", [P_NODE, ZF])
        spare = sb("spare", [P, 1])
        spare1 = sb("spare1", [P, 1])
        spare_i = sb("spare_i", [P, 1], I32)
        ident = sb("ident", [P, P])
        iota_f = sb("iota_f", [P, WINDOW])
        ones_row = sb("ones_row", [1, P])
        zero_row = sb("zero_row", [1, P], BF16)
        last_row = sb("last_row", [1, D + 1])
        half = sb("half", [P, 1])
        spill = sb("spill", [P, 8])
        spill_i = sb("spill_i", [1, 1], I32)
        stats = sb("stats", [P_NODE, BLOCKS, 6])
        mean = sb("mean", [P_NODE, BLOCKS])
        rstd = sb("rstd", [P_NODE, BLOCKS])
        rs_deg = sb("rs_deg", [P_NODE, BLOCKS])
        rc_deg = sb("rc_deg", [P_NODE, BLOCKS])
        rq_v = sb("rq_v", [P, max(BLOCKS, D)])
        rq_l = sb("rq_l", [P, max(BLOCKS, D)])
        rq_y = sb("rq_y", [P, max(BLOCKS, D)])
        rq_t = sb("rq_t", [P, max(BLOCKS, D)])
        bn_raw = sb("bn_raw", [P, NC, 6])
        bn_mv = sb("bn_mv", [P, 2])
        bn_sc = sb("bn_sc", [P, 1])
        bn_sh = sb("bn_sh", [P, 1])
        bn_t = sb("bn_t", [P, 1])

        We1 = sb("We1", [P, P])
        We2 = sb("We2", [P, P])
        be2x = sb("be2x", [1, 4 * D])
        be1 = sb("be1", [P, 2])
        Wn = sb("Wn", [D + 1, D])
        Wc = sb("Wc", [D, P])
        bc = sb("bc", [D, 2])
        Wo = sb("Wo", [D + 1, D])
        gin_W1 = sb("gin_W1", [D, P])
        gin_W2 = sb("gin_W2", [P, D])
        gin_v1 = sb("gin_v1", [P, 3])
        gin_v2 = sb("gin_v2", [D, 3])
        gin_eps = sb("gin_eps", [D, 1])
        bi_W1 = sb("bi_W1", [D, D])
        bi_W2 = sb("bi_W2", [D, D])
        Wp = sb("Wp", [D + 1, D])
        Wu = sb("Wu", [D + 1, D])
        Wu_agg = sb("Wu_agg", [D, D])
        rows3 = sb("rows3", [1, 8, D])
        fold = sb("fold", [1, 4, D])

        gath_all = sb("gath", [P, SLOTS * TILES * D])
        gath = [gath_all[:, s * TILES * D:(s + 1) * TILES * D] for s in range(SLOTS)]
        idx = [sb(f"idx{s}", [P, TILES], I32) for s in range(SLOTS)]
        onehot = [sb(f"onehot{s}", [P, TILES * WINDOW]) for s in range(SLOTS)]
        one_p = [sb(f"one_p{s}", [P, TILES, P], BF16) for s in range(SLOTS)]
        one_b = [sb(f"one_b{s}", [P, TILES, BLOCKS], BF16) for s in range(SLOTS)]
        wdst = sb("wdst", [P, TILES])

        def shared(kind, s):
            o = (kind * SLOTS + s) * TILES * D
            return hT[:, o:o + TILES * D]

        eat = [shared(0, s) for s in range(SLOTS)]
        eaT = [shared(1, s) for s in range(SLOTS)]
        u1 = [shared(2, s) for s in range(SLOTS)]
        a1 = [shared(3, s) for s in range(SLOTS)]
        u2 = [shared(4, s) for s in range(SLOTS)]
        filt = [shared(5, s) for s in range(SLOTS)]

        hn = [sb(f"hn{k}", [P_NODE, CF]) for k in range(2)]
        hs = [sb(f"hs{k}", [P_NODE, CF]) for k in range(2)]
        tab = [sb(f"tab{k}", [P_NODE, CF]) for k in range(2)]
        col = [sb(f"col{k}", [D + 1, CN]) for k in range(2)]
        gcol = [onehot[k][:, 0:CN] for k in range(2)]
        hgcol = [onehot[2][:, 0:CN], gath_all[:, 0:CN]]

        def in_agg(kind, s):
            o = (kind * SLOTS + s) * TILES * P
            return aggT[:, o:o + TILES * P]

        same = [in_agg(0, s) for s in range(SLOTS)]
        diag = onehot
        total = [in_agg(1, s)[:, 0:TILES * D] for s in range(SLOTS)]
        later = [sb(f"later{s}", [P, TILES]) for s in range(SLOTS)]
        to_idx = [sb(f"to_idx{s}", [P, TILES], I32) for s in range(SLOTS)]
        part = [[in_agg(2, k)[0:P_NODE, 0:CF], in_agg(2, k)[0:P_NODE, CF:2 * CF],
                 in_agg(3, k)[0:P_NODE, 0:CF], in_agg(3, k)[0:P_NODE, CF:2 * CF]] for k in range(2)]

        def row_view(a, q):
            o = (a * GR + q) * STEP
            return aggT[:, o:o + STEP] if a == 2 else aggT[:, o:o + STEP].bitcast(I32)

        def row_float(a, q):
            o = (a * GR + q) * STEP
            return aggT[:, o:o + STEP] if a == 2 else hT[:, o:o + STEP]

        iota_i = gath_all[:, 0:WINDOW].bitcast(I32)
        sp_q = hT[:, G * TILES:2 * G * TILES]
        sp_r = aggT[:, 0:G * TILES]
        sp_t = aggT[:, G * TILES:2 * G * TILES]
        sp_i = aggT[:, 2 * G * TILES:3 * G * TILES].bitcast(I32)

        ps = [bank(f"ps{i}", [P, 512]) for i in range(8)]
        ps_eT, ps_z1, ps_z2 = ps[0][:, 0:256], ps[1][:, 0:256], ps[2][:, 0:256]
        ps_agg = [ps[3 + s][0:D, 0:WINDOW] for s in range(SLOTS)]
        ps_count = ps[6][0:P_NODE, 0:BLOCKS]
        ps_src = [ps[s] for s in range(SLOTS)]
        ps_total = [ps[3 + s][:, 0:TILES * D] for s in range(SLOTS)]

        s_x = sem("x_loaded")
        s_w = sem("weights_loaded")
        s_rows = sem("edge_rows_loaded")
        s_pad = sem("padding_written")
        s_iota = sem("iota_written")
        s_zero = sem("weights_zeroed")
        s_const = sem("constants_written")
        s_ident = sem("identity_written")
        s_rowf = sem("edge_rows_as_float")
        s_rowT = sem("edge_rows_transposed")
        s_list = sem("edge_lists_written")
        s_setup = sem("vector_setup_step")
        s_dstf = sem("dst_as_float")
        s_baseb = sem("bases_broadcast")
        s_flags = sem("spill_flags_written")
        s_flagT = sem("spill_flags_transposed")
        s_spill = sem("spill_flag_ready")
        s_rqv = sem("rsqrt_argument_ready")
        s_rqy = sem("rsqrt_guess_ready")
        s_rqn = sem("rsqrt_newton_step")
        s_fold = sem("bn_fold_rows_ready")
        s_foldb = sem("bn_fold_broadcast")
        s_ready = sem("weights_ready")
        s_stat = sem("layernorm_stats")
        s_hn = sem("normalised_chunk")
        s_hs = sem("relu_chunk")
        s_tT = sem("chunk_transposed")
        s_hT = sem("feature_major_kept")
        s_col = sem("feature_major_staged")
        s_proj = sem("table_projected")
        s_tab = sem("table_chunk_ready")
        s_tdma = [sem(f"table_chunk_stored{k}") for k in range(2)]
        s_idx = sem("indices_staged")
        s_gath = [[sem(f"rows_gathered_L{L}_{s}") for s in range(SLOTS)] for L in range(4)]
        s_go = sem("waits_carried")
        s_ea = [sem(f"edge_attr_loaded{s}") for s in range(SLOTS)]
        s_eT = sem("edge_attr_transposed")
        s_eTc = sem("edge_attr_T_copied")
        s_z1 = sem("z1_ready")
        s_m1 = sem("z1_clamped")
        s_e1 = sem("exp1_done")
        s_l1 = sem("log1_done")
        s_a1 = sem("a1_ready")
        s_z2 = sem("z2_ready")
        s_m2 = sem("z2_clamped")
        s_e2 = sem("exp2_done")
        s_l2 = sem("log2_done")
        s_f = sem("filter_ready")
        s_msg = sem("messages_ready")
        s_oh = sem("onehot_ready")
        s_agg = sem("window_summed")
        s_added = sem("window_added")
        s_cntoh = sem("count_onehots_ready")
        s_cnt = sem("count_step_summed")
        s_cntall = sem("count_complete")
        s_goh = sem("general_onehot_ready")
        s_gsum = sem("general_window_summed")
        s_gadd = sem("general_window_added")
        s_gdst = sem("general_dst_shifted")
        s_aggdone = sem("layer_aggregated")
        s_zeroed = sem("accumulators_zeroed")
        s_prep3 = sem("layer3_lists_ready")
        s_diag = sem("src_diagonals_ready")
        s_bsrc = sem("src_broadcast")
        s_same = sem("same_src_ready")
        s_dup = sem("duplicates_redirected")
        s_to = sem("scatter_rows_ready")
        s_wrow = sem("weighted_rows_ready")
        s_tot = sem("row_totals_summed")
        s_totc = sem("row_totals_copied")
        s_scat = [sem(f"rows_scattered{s}") for s in range(SLOTS)]
        s_part = [sem(f"accumulators_loaded{k}") for k in range(2)]
        s_psum = sem("accumulators_added")
        s_pavg = sem("average_ready")
        s_pT = sem("average_transposed")
        s_pTc = sem("average_staged")
        s_pa = sem("conv_product_ready")
        s_pm = sem("conv_clamped")
        s_pe = sem("conv_exp")
        s_pl = sem("conv_log")
        s_sp = sem("conv_softplus")
        s_pb = sem("layer_products_ready")
        s_px = sem("residual_added")
        s_comb = sem("combined_ready")
        s_h1 = sem("gin_hidden_product")
        s_bn = sem("batchnorm_stats")
        s_bnc = sem("batchnorm_constants")
        s_h1b = sem("gin_hidden_again")
        s_act1 = sem("gin_hidden_activated")
        s_h2 = sem("gin_second_product")
        s_h2k = sem("gin_second_kept")
        s_y = sem("gin_output_scaled")
        s_yT = sem("gin_output_transposed")
        s_stg = sem("operands_staged")
        s_hg = sem("h_times_sum")
        s_t1 = sem("neighbour_term_scaled")
        s_t2 = sem("terms_summed")
        s_t3 = sem("leaky_relu_done")
        s_out = sem("output_stored")

        block = ctx.enter_context(nc.Block())

        def agg_chunk(c):
            return aggT[0:D, 0:N].rearrange("k (p b) -> k b p", b=BLOCKS)[:, bass.ds(c * CB, CB), :]

        def hT_chunk(c):
            return hT[0:D, bass.ds(c * CN, CN)]

        def x_chunk(c):
            return x_nm[:, bass.ds(c * CF, CF)]

        def by_block(ap):
            return ap.rearrange("k (a b) -> k a b", a=CB)

        def by_tile(ap):
            return ap.rearrange("p (g j) -> p g j", j=TILES)

        def spread(ap, n):
            return ap.rearrange("p (a o) -> p a o", o=1).to_broadcast([ap.shape[0], ap.shape[1], n])

        def table_uses(k, L, rnd=0):
            return L * ((NC + 1 - k) // 2) + rnd

        def gathered(eng, L, g):
            eng.wait_ge(s_gath[L][g.slot], 16 * TILES * (g.round + 1))

        def wait_for(eng, s, n):
            if not (isinstance(n, int) and n <= 0):
                eng.wait_ge(s, n)

        @block.sync
        def _(sp):
            sp.wait_ge(s_pad, 3)
            for a, name in enumerate(("src", "dst", "edge_weight")):
                for q in range(GR):
                    rows = min(P, G - 1 - q * P)
                    if rows > 0:
                        sp.dma_start(row_view(a, q)[0:rows, :],
                                     io[name][q * P * STEP:(q * P + rows) * STEP].rearrange("(g e) -> g e", e=STEP))\
                          .then_inc(s_rows, 16)
                r = (G - 1) % P
                sp.dma_start(row_view(a, GR - 1)[r:r + 1, 0:TAIL],
                             io[name][(G - 1) * STEP:E].rearrange("(o e) -> o e", o=1)).then_inc(s_rows, 16)
            xd = io["x"].rearrange("(p b) d -> p (b d)", b=BLOCKS)
            sp.dma_start(x_nm[0:112, :], xd[0:112, :]).then_inc(s_x, 16)
            sp.dma_start(x_nm[112:P_NODE, :], xd[112:P_NODE, :]).then_inc(s_x, 16)

            def store_table(L):
                to = table[L].rearrange("(p b) d -> p (b d)", b=BLOCKS)

                def body(at):
                    c = at(0)
                    sp.wait_ge(s_tab, L * NC + c.n + 3)
                    sp.dma_start(to[:, bass.ds(c.n * CF, CF)], tab[c.slot][:, :]).then_inc(s_tdma[c.slot], 16)
                turns(sp, NC, 2, 0, 0, body)

            store_table(0)
            ea = io["edge_attr_64"]
            rows = ea[0:(G - 1) * STEP, :].rearrange("(r j) d -> r (j d)", j=TILES)
            sp.wait_ge(s_ready, 1)

            def load_attr(at):
                g = at(0)
                sp.wait_ge(s_eT, g.n + 1)
                sp.dma_start(eat[g.slot], rows[bass.ds(g.n * P, P), :]).then_inc(s_ea[g.slot], 16)
            turns(sp, G - 1, SLOTS, 0, 0, load_attr)
            last = Item(0, G - 1, SLOTS)
            sp.wait_ge(s_eT, last.n + 1)
            sp.dma_start(eat[last.slot][0:TAIL // TILES, :],
                         ea[(G - 1) * STEP:E, :].rearrange("(r j) d -> r (j d)", j=TILES)).then_inc(s_ea[last.slot], 16)
            sp.wait_ge(s_zero, 1)
            for j in range(TILES):
                to = acc[j].rearrange("(n p b) d -> n p (b d)", p=P_NODE, b=4)

                def store_zeros(at, to=to):
                    z = at(0)
                    sp.dma_start(to[bass.ds(z.n, 1), :, :].rearrange("o p f -> (o p) f"), zeros[:, :])\
                      .then_inc(s_zeroed, 16)
                turns(sp, (N + SPARE) // (4 * P_NODE), 1, 0, 0, store_zeros)
            for L in (1, 2, 3):
                store_table(L)
            sp.wait_ge(s_aggdone, 4)
            views = [acc[j][0:N, :].rearrange("(p b) d -> p (b d)", b=BLOCKS) for j in range(TILES)]

            def load_parts(at):
                c = at(0)
                sp.wait_ge(s_pavg, c.n + 1)
                for j in range(TILES):
                    sp.dma_start(part[c.slot][j], views[j][:, bass.ds(c.n * CF, CF)]).then_inc(s_part[c.slot], 16)
            turns(sp, NC, 2, 0, 0, load_parts)
            sp.wait_ge(s_px, 2 + 4 * NC)
            od = io["out"].rearrange("(p b) d -> p (b d)", b=BLOCKS)
            sp.dma_start(od[0:112, :], x_nm[0:112, :]).then_inc(s_out, 16)
            sp.dma_start(od[112:P_NODE, :], x_nm[112:P_NODE, :]).then_inc(s_out, 16)
            sp.wait_ge(s_out, 32)

        @block.gpsimd
        def _(pool):
            for a in range(2):
                nc.gpsimd.memset(row_view(a, GR - 1), -1).then_inc(s_pad, 1)
            nc.gpsimd.memset(row_view(2, GR - 1), 0.0).then_inc(s_pad, 1)
            nc.gpsimd.iota(iota_i, [[1, WINDOW]], base=0, channel_multiplier=0).then_inc(s_iota, 1)
            nc.gpsimd.memset(ident[:, :], 0.0).then_inc(s_ident, 1)
            pool.wait_ge(s_ident, 1)
            nc.gpsimd.affine_select(out=ident[:, :], in_=ident[:, :], compare_op=ALU.not_equal, fill=1.0,
                                    base=0, pattern=[[-1, P]], channel_multiplier=1).then_inc(s_ident, 1)
            nc.gpsimd.memset(upper[:, :], 1.0).then_inc(s_ident, 1)
            nc.gpsimd.iota(spare_i[:, :], [[0, 1]], base=N, channel_multiplier=1).then_inc(s_iota, 1)
            pool.wait_ge(s_ident, 3)
            nc.gpsimd.affine_select(out=upper[:, :], in_=upper[:, :], compare_op=ALU.is_ge, fill=0.0,
                                    base=0, pattern=[[1, P]], channel_multiplier=-1).then_inc(s_ident, 1)
            for L in range(3):
                for k in range(2):
                    pool.wait_ge(s_tdma[k], 16 * table_uses(k, L + 1))

                def gather(at, L=L):
                    g = at(0)
                    pool.wait_ge(s_idx, L * G + g.n + 1)
                    if L == 0:
                        pool.wait_ge(s_msg, g.n + 1)
                    else:
                        pool.wait_ge(s_agg, L * G + g.n + 1)
                    pool.sem_inc(s_go, 1)
                    for j in range(TILES):
                        nc.gpsimd.indirect_dma_start(
                            out=gath[g.slot][:, j * D:(j + 1) * D], out_offset=None, in_=table[L][:, :],
                            in_offset=bass.IndirectOffsetOnAxis(ap=idx[g.slot][:, j:j + 1], axis=0),
                        ).then_inc(s_gath[L][g.slot], 16)
                turns(pool, G, SLOTS, 0, 0, gather)

            for k in range(2):
                pool.wait_ge(s_tdma[k], 16 * table_uses(k, 4))
            pool.wait_ge(s_zeroed, 16 * TILES * ((N + SPARE) // (4 * P_NODE)))

            def gather_scatter(at):
                g, ahead = at(0), at(1)
                if ahead:
                    pool.wait_ge(s_idx, 3 * G + ahead.n + 1)
                    pool.wait_ge(s_tot, ahead.n + 1)
                    pool.sem_inc(s_go, 1)
                    for j in range(TILES):
                        nc.gpsimd.indirect_dma_start(
                            out=gath[ahead.slot][:, j * D:(j + 1) * D], out_offset=None, in_=table[3][:, :],
                            in_offset=bass.IndirectOffsetOnAxis(ap=idx[ahead.slot][:, j:j + 1], axis=0),
                        ).then_inc(s_gath[3][ahead.slot], 16)
                if g:
                    prev = at(-1)
                    pool.wait_ge(s_to, g.n + 1)
                    pool.wait_ge(s_totc, SLOTS + g.n + 1)
                    if prev:
                        pool.wait_ge(s_scat[prev.slot], 16 * TILES * (prev.round + 1))
                    pool.sem_inc(s_go, 1)
                    for j in range(TILES):
                        nc.gpsimd.indirect_dma_start(
                            out=acc[j][:, :],
                            out_offset=bass.IndirectOffsetOnAxis(ap=to_idx[g.slot][:, j:j + 1], axis=0),
                            in_=total[g.slot][:, j * D:(j + 1) * D], in_offset=None, compute_op=ALU.add,
                        ).then_inc(s_scat[g.slot], 16)
            turns(pool, G, SLOTS, 1, 0, gather_scatter, peel=1)

        @block.scalar
        def _(act):
            def load(to, name_or_ap):
                ap = io[name_or_ap] if isinstance(name_or_ap, str) else name_or_ap
                act.dma_start(to, ap).then_inc(s_w, 16)

            def as_col(name):
                return io[name].rearrange("(p o) -> p o", o=1)

            def as_row(name):
                return io[name].rearrange("(o d) -> o d", o=1)

            act.wait_ge(s_zero, 1)
            for o in (0, D):
                load(We1[o:o + D, o:o + D], "L0_gnn_We1")
                load(We2[o:o + D, o:o + D], "L0_gnn_We2")
                load(be1[o:o + D, 0:1], as_col("L0_gnn_be1"))
            for r in range(4):
                load(be2x[0:1, r * D:(r + 1) * D], as_row("L0_gnn_be2"))
            load(Wn[0:D, :], "L0_gnn_Wn")
            load(Wn[D:D + 1, :], as_row("L0_gnn_bn"))
            load(Wc[:, 0:D], "L0_gnn_Wc")
            load(bc[:, 0:1], as_col("L0_gnn_bc"))
            load(Wo[0:D, :], "L0_gnn_Wo")
            load(Wo[D:D + 1, :], as_row("L0_gnn_bo"))
            load(gin_W1[:, :], "L1_gnn_W1")
            load(gin_W2[:, :], "L1_gnn_W2")
            for i, v in enumerate(("b", "g", "be")):
                load(gin_v1[:, i:i + 1], as_col(f"L1_gnn_{v}1"))
                load(gin_v2[:, i:i + 1], as_col(f"L1_gnn_{v}2"))
            load(gin_eps[:, :], io["L1_gnn_epsilon"].to_broadcast([D, 1]))
            load(bi_W1[:, :], "L2_gnn_W1")
            load(bi_W2[:, :], "L2_gnn_W2")
            load(Wp[0:D, :], "L3_gnn_W_prep")
            load(Wp[D:D + 1, :], as_row("L3_gnn_b_prep"))
            load(Wu[0:D, :], io["L3_gnn_W_upd"][0:D, :])
            load(Wu[D:D + 1, :], as_row("L3_gnn_b_upd"))
            load(Wu_agg[:, :], io["L3_gnn_W_upd"][D:2 * D, :])
            for i, v in enumerate(("gamma_p", "beta_p", "mean_p", "var_p", "gamma_u", "beta_u", "mean_u", "var_u")):
                load(rows3[0:1, i, :], as_row(f"L3_gnn_{v}"))
            guesses = [0]

            def rsqrt_guess(rows, cols):
                guesses[0] += 1
                n = guesses[0]
                act.wait_ge(s_rqv, n)
                act.activation(rq_l[0:rows, 0:cols], rq_v[0:rows, 0:cols], ACT.Ln).then_inc(s_rqy, 1)
                act.wait_ge(s_rqy, 2 * n - 1)
                act.activation(rq_y[0:rows, 0:cols], rq_l[0:rows, 0:cols], ACT.Exp, scale=-0.5).then_inc(s_rqy, 1)

            rsqrt_guess(1, D)
            rsqrt_guess(1, D)

            def make_table(L):
                rsqrt_guess(P_NODE, BLOCKS)

                def body(at):
                    c, e = at(1), at(0)
                    if c:
                        n = L * NC + c.n
                        act.wait_ge(s_hn, n + 1)
                        if L == 1:
                            wait_for(act, s_tdma[c.slot], 16 * table_uses(c.slot, L, c.round))
                            act.activation(tab[c.slot][:, :], hn[c.slot][:, :], ACT.Relu).then_inc(s_tab, 1)
                        act.wait_ge(s_tT, n + 1)
                        if L == 2:
                            act.wait_ge(s_tab, n + 1)
                        act.activation(hs[c.slot][:, :], hn[c.slot][:, :], ACT.Relu).then_inc(s_hs, 1)
                    if e:
                        n = L * NC + e.n
                        if L:
                            act.wait_ge(s_tT, n + 3)
                            if L == 3:
                                act.wait_ge(s_col, NC + e.n + 3)
                            act.activation(hT_chunk(e.n), ps[e.slot][0:D, 0:CN], ACT.Copy).then_inc(s_hT, 1)
                        if L in (0, 3):
                            act.wait_ge(s_proj, (L // 3) * NC + e.n + 3)
                            wait_for(act, s_tdma[e.slot], 16 * table_uses(e.slot, L, e.round))
                            act.activation(tab[e.slot][:, :], ps[2 + e.slot][0:P_NODE, 0:CF],
                                           ACT.Relu if L else ACT.Copy).then_inc(s_tab, 1)
                turns(act, NC, 2, 1, 0, body, peel=1)

            def stage_indices(g, of=src_f):
                act.activation(idx[g.slot][:, :], of[:, bass.ds(g.n * TILES, TILES)], ACT.Relu).then_inc(s_idx, 1)

            def stage_first(L):
                for s in range(SLOTS):
                    if L:
                        gathered(act, L - 1, Item(0, G - 1 - (G - 1 - s) % SLOTS, SLOTS))
                    stage_indices(Item(0, s, SLOTS), dst_f if L == 3 else src_f)

            make_table(0)
            stage_first(0)

            def filter_steps(at):
                g0, g1, g2, g3 = (at(o) for o in range(4))
                if g1:
                    act.wait_ge(s_m2, g1.n + 1)
                    act.activation(u2[g1.slot], u2[g1.slot], ACT.Exp).then_inc(s_e2, 1)
                    act.wait_ge(s_e2, g1.n + 1)
                    act.activation(u2[g1.slot], u2[g1.slot], ACT.Ln, bias=half[:, :], scale=0.5).then_inc(s_l2, 1)
                if g2:
                    act.wait_ge(s_m1, g2.n + 1)
                    act.activation(u1[g2.slot], u1[g2.slot], ACT.Exp).then_inc(s_e1, 1)
                    act.wait_ge(s_e1, g2.n + 1)
                    act.activation(u1[g2.slot], u1[g2.slot], ACT.Ln, bias=half[:, :], scale=0.5).then_inc(s_l1, 1)
                if g3:
                    act.wait_ge(s_eT, SLOTS + g3.n + 1)
                    act.activation(eaT[g3.slot], ps_eT, ACT.Copy).then_inc(s_eTc, 1)
                if g0 and g3:
                    gathered(act, 0, g0)
                    stage_indices(g3)
            turns(act, G, SLOTS, 3, 0, filter_steps)

            def post0(at):
                c = at(0)
                act.wait_ge(s_pm, c.n + 1)
                act.activation(gcol[c.slot][0:D, :], gcol[c.slot][0:D, :], ACT.Exp).then_inc(s_pe, 1)
                act.wait_ge(s_pe, c.n + 1)
                act.activation(gcol[c.slot][0:D, :], gcol[c.slot][0:D, :], ACT.Ln, bias=half[0:D, :], scale=0.5)\
                   .then_inc(s_pl, 1)
            turns(act, NC, 2, 0, 0, post0)
            make_table(1)

            def plain_steps(L):
                stage_first(L)

                def body(at):
                    g0, g3 = at(0), at(3)
                    if g0 and g3:
                        gathered(act, L, g0)
                        stage_indices(g3)
                turns(act, G, SLOTS, 3, 0, body)

            plain_steps(1)
            rsqrt_guess(P_NODE, BLOCKS)
            rsqrt_guess(P, 1)
            act.wait_ge(s_bnc, 1)

            def hidden(at):
                c = at(0)
                act.wait_ge(s_h1b, c.n + 1)
                act.wait_ge(s_h2, c.n + 1)
                act.activation(gcol[c.slot][:, :], ps[c.slot][:, 0:CN], ACT.Relu, bias=bn_sh[:, :],
                               scale=bn_sc[:, :]).then_inc(s_act1, 1)
            turns(act, NC, 2, 0, 0, hidden)
            rsqrt_guess(D, 1)
            act.wait_ge(s_bnc, 2)

            def gin_output(at):
                c = at(0)
                act.wait_ge(s_yT, c.n + 1)
                act.activation(col[c.slot][0:D, :], hT_chunk(c.n), ACT.Identity, bias=bn_sh[0:D, :],
                               scale=bn_sc[0:D, :]).then_inc(s_y, 1)
            turns(act, NC, 2, 0, 0, gin_output)
            make_table(2)
            plain_steps(2)

            act.wait_ge(s_aggdone, 3)

            def stage_operands(at):
                c = at(0)
                act.wait_ge(s_pb, NC + c.n + 1)
                act.activation(col[c.slot][0:D, :], hT_chunk(c.n), ACT.Copy)
                act.activation(by_block(gcol[c.slot][0:D, :]), agg_chunk(c.n), ACT.Copy).then_inc(s_stg, 1)
            turns(act, NC, 2, 0, 0, stage_operands)
            make_table(3)
            stage_first(3)

            def total_steps(at):
                g, ahead = at(0), at(3)
                if g:
                    act.wait_ge(s_tot, SLOTS + g.n + 1)
                    wait_for(act, s_scat[g.slot], 16 * TILES * g.round)
                    act.activation(total[g.slot], ps_total[g.slot], ACT.Copy).then_inc(s_totc, 1)
                    if ahead:
                        gathered(act, 3, g)
                        stage_indices(ahead, dst_f)
            turns(act, G, SLOTS, 3, 0, total_steps, peel=1)

            def stage_update(at):
                c = at(0)
                act.wait_ge(s_pb, 2 * NC + c.n + 1)
                act.activation(col[c.slot][0:D, :], hT_chunk(c.n), ACT.Copy).then_inc(s_stg, 1)
                act.wait_ge(s_pT, c.n + 1)
                act.activation(gcol[c.slot][0:D, :], ps[4 + c.slot][0:D, 0:CN], ACT.Copy).then_inc(s_pTc, 1)
            turns(act, NC, 2, 0, 0, stage_update)

        @block.vector
        def _(dve):
            V = nc.vector
            step = [0]

            def link(ins):
                step[0] += 1
                ins.then_inc(s_setup, 1)
                dve.wait_ge(s_setup, step[0])

            for w in (We1, We2, zeros):
                V.memset(w[:, :], 0.0)
            V.memset(Wc[:, :], 0.0).then_inc(s_zero, 1)
            V.memset(last_row[:, 0:D], 0.0)
            V.memset(last_row[:, D:D + 1], 1.0)
            V.memset(ones_row[:, :], 1.0)
            V.memset(ones_pp[:, :], 1.0)
            V.memset(zero_row[:, :], 0.0)
            V.memset(half[:, :], 0.5)
            for k in range(2):
                V.memset(col[k][D:D + 1, :], 1.0)
            V.memset(spill[:, :], 0.0).then_inc(s_const, 1)
            for s in (s_hs, s_tT, s_hT, s_col, s_proj, s_tab, s_sp, s_pb, s_px, s_bn, s_act1, s_h2, s_h2k, s_yT, s_t2, s_pavg):
                dve.sem_inc(s, 2)
            for s in (s_eT, s_msg, s_agg, s_added, s_cnt, s_same, s_tot, s_totc):
                dve.sem_inc(s, SLOTS)
            dve.wait_ge(s_ident, 4)
            dve.wait_ge(s_iota, 2)
            link(V.tensor_copy(iota_f[:, :], iota_i))
            link(V.tensor_copy(spare[:, :], spare_i[:, :]))
            link(V.tensor_scalar(spare1[:, :], spare[:, :], 1.0, None, ALU.add))

            dve.wait_ge(s_rows, 16 * 3 * (-(-(G - 1) // P) + 1))
            for a in range(2):
                for q in range(GR):
                    r = min(P, G - q * P)
                    V.tensor_copy(row_float(a, q)[0:r, :], row_view(a, q)[0:r, :]).then_inc(s_rowf, 1)
            lists = (src_f, dst_f, w_edge)
            for i in range(3 * GR):
                a, q = i // GR, i % GR
                r = min(P, G - q * P)
                dve.wait_ge(s_rowT, i + 1)
                V.tensor_copy(by_tile(lists[a][:, :]).rearrange("p g j -> p j g")[:, :, q * P:q * P + r],
                              ps[i % 2][:, :].rearrange("p (j g) -> p j g", j=TILES)[:, :, 0:r]).then_inc(s_list, 1)
            dve.wait_ge(s_list, 3 * GR)
            V.tensor_copy(base_i[0:1, :], by_tile(dst_f[:, :])[0:1, :, 0]).then_inc(s_dstf, 1)
            dve.wait_ge(s_baseb, 1)
            link(V.tensor_tensor(by_tile(dst_rel[:, :]), by_tile(dst_f[:, :]), spread(ps[2][:, 0:G], TILES), ALU.subtract))
            link(V.tensor_scalar(sp_t, dst_rel[:, :], float(WINDOW), None, ALU.is_ge))
            link(V.tensor_reduce(spill[:, 0:1], sp_t, AX.X, ALU.max))
            link(V.tensor_scalar(sp_t, dst_rel[:, :], 0.0, None, ALU.is_lt))
            link(V.scalar_tensor_tensor(sp_t, dst_f[:, :], 0.0, sp_t, ALU.is_ge, ALU.mult))
            link(V.tensor_reduce(spill[:, 1:2], sp_t, AX.X, ALU.max))
            V.tensor_tensor(spill[:, 2:3], spill[:, 0:1], spill[:, 1:2], ALU.max).then_inc(s_flags, 1)
            dve.wait_ge(s_flagT, 1)
            link(V.tensor_reduce(spill[0:1, 4:5], ps[3][0:1, 0:P], AX.X, ALU.max))
            V.tensor_copy(spill_i[:, :], spill[0:1, 4:5]).then_inc(s_spill, 1)
            v = src_f[:, :]
            link(V.tensor_scalar(sp_i, v, 1.0 / BLOCKS, None, ALU.mult))
            link(V.tensor_copy(sp_q, sp_i))
            link(V.scalar_tensor_tensor(sp_r, sp_q, -float(BLOCKS), v, ALU.mult, ALU.add))
            link(V.tensor_scalar(sp_t, sp_r, 0.0, None, ALU.is_lt))
            link(V.tensor_tensor(sp_q, sp_q, sp_t, ALU.subtract))
            link(V.scalar_tensor_tensor(sp_r, sp_t, float(BLOCKS), sp_r, ALU.mult, ALU.add))
            link(V.tensor_scalar(sp_t, sp_r, float(BLOCKS), None, ALU.is_ge))
            link(V.tensor_tensor(node_p, sp_q, sp_t, ALU.add))
            link(V.scalar_tensor_tensor(node_b, sp_t, -float(BLOCKS), sp_r, ALU.mult, ALU.add))

            rq = [0, 0]

            def rsqrt(rows, cols, out):
                rq[0] += 1
                dve.wait_ge(s_rqy, 2 * rq[0])
                v, y, t = (z[0:rows, 0:cols] for z in (rq_v, rq_y, rq_t))

                def newton(ins):
                    rq[1] += 1
                    ins.then_inc(s_rqn, 1)
                    dve.wait_ge(s_rqn, rq[1])
                newton(V.tensor_tensor(t, y, y, ALU.mult))
                newton(V.tensor_tensor(t, t, v, ALU.mult))
                newton(V.tensor_scalar(t, t, -0.5, 1.5, ALU.mult, ALU.add))
                newton(V.tensor_tensor(out, y, t, ALU.mult))

            dve.wait_ge(s_w, 16 * 40)
            link(V.tensor_scalar(be1[:, 1:2], be1[:, 0:1], -LOG2, None, ALU.add))
            link(V.tensor_scalar(bc[:, 1:2], bc[:, 0:1], -LOG2, None, ALU.add))
            for i in range(2):
                gamma, beta, mu, var = (rows3[0:1, 4 * i + j, :] for j in range(4))
                scale, shift, t = fold[0:1, 2 * i, :], fold[0:1, 2 * i + 1, :], rq_t[0:1, 0:D]
                V.tensor_scalar(rq_v[0:1, 0:D], var, BN3_EPS, None, ALU.add).then_inc(s_rqv, 1)
                rsqrt(1, D, scale)
                link(V.tensor_tensor(scale, scale, gamma, ALU.mult))
                link(V.tensor_tensor(t, mu, scale, ALU.mult))
                link(V.tensor_tensor(shift, beta, t, ALU.subtract))
            dve.sem_inc(s_fold, 1)
            dve.wait_ge(s_foldb, 1)
            for i, w in enumerate((Wp, Wu)):
                link(V.tensor_tensor(w[:, :], w[:, :], ps[4][0:D + 1, P * i:P * i + D], ALU.mult))
                link(V.tensor_tensor(w[:, :], w[:, :], ps[5][0:D + 1, P * i:P * i + D], ALU.add))
            link(V.tensor_tensor(Wu_agg[:, :], Wu_agg[:, :], ps[4][0:D, P:P + D], ALU.mult))
            link(V.memset(aggT[0:D, 0:N + WINDOW], 0.0))
            dve.sem_inc(s_added, 1)
            dve.sem_inc(s_ready, 1)

            def make_table(L):
                dve.wait_ge(s_px, 2 + L * NC)

                def layer_stats(at):
                    c = at(0)
                    for j in range(CB):
                        b = c.n * CB + j
                        ins = V.bn_stats(stats[:, bass.ds(b, 1), :].rearrange("p o s -> p (o s)"),
                                         x_nm[:, bass.ds(b * D, D)])
                    ins.then_inc(s_stat, 1)
                turns(dve, NC, 2, 0, 0, layer_stats)
                dve.wait_ge(s_stat, (L + 1) * NC)
                v = rq_v[0:P_NODE, 0:BLOCKS]
                link(V.tensor_tensor(mean[:, :], stats[:, :, 1], stats[:, :, 4], ALU.add))
                link(V.tensor_tensor(rstd[:, :], stats[:, :, 1], stats[:, :, 4], ALU.subtract))
                link(V.tensor_scalar(mean[:, :], mean[:, :], 0.5, None, ALU.mult))
                link(V.tensor_tensor(rstd[:, :], rstd[:, :], rstd[:, :], ALU.mult))
                link(V.tensor_tensor(v, stats[:, :, 2], stats[:, :, 5], ALU.add))
                link(V.tensor_scalar(v, v, 1.0 / D, LN_EPS, ALU.mult, ALU.add))
                V.scalar_tensor_tensor(v, rstd[:, :], 0.25, v, ALU.mult, ALU.add).then_inc(s_rqv, 1)
                rsqrt(P_NODE, BLOCKS, rstd[:, :])

                def body(at):
                    c, e = at(1), at(0)
                    if c:
                        dve.wait_ge(s_hs, L * NC + c.n + 1)
                        for j in range(CB):
                            b = c.n * CB + j
                            ins = V.tensor_scalar(hn[c.slot][:, j * D:(j + 1) * D], x_nm[:, bass.ds(b * D, D)],
                                                  mean[:, bass.ds(b, 1)], rstd[:, bass.ds(b, 1)],
                                                  ALU.subtract, ALU.mult)
                        ins.then_inc(s_hn, 1)
                    if e and L in (0, 3):
                        m = (L // 3) * NC + e.n
                        dve.wait_ge(s_tT, L * NC + e.n + 3)
                        dve.wait_ge(s_proj, m + 1)
                        V.tensor_copy(col[e.slot][0:D, :], ps[e.slot][0:D, 0:CN]).then_inc(s_col, 1)
                    if e and L == 2:
                        dve.wait_ge(s_hs, L * NC + e.n + 3)
                        dve.wait_ge(s_tdma[e.slot], 16 * table_uses(e.slot, L, e.round))
                        V.tensor_tensor(by_block(tab[e.slot][:, :]), by_block(hs[e.slot][:, :]),
                                        spread(rs_deg[:, bass.ds(e.n * CB, CB)], D), ALU.mult).then_inc(s_tab, 1)
                turns(dve, NC, 2, 1, 0, body)

            dve.wait_ge(s_x, 32)
            make_table(0)
            dve.wait_ge(s_spill, 1)
            spilled = dve.value_load(spill_i[0:1, 0:1], min_val=0, max_val=1)

            def dst_onehots(to, dst, at):
                for j in range(TILES):
                    ins = V.tensor_scalar(to[:, j * WINDOW:(j + 1) * WINDOW], iota_f[:, :], dst[:, bass.ds(at + j, 1)],
                                          None, ALU.is_equal)
                return ins

            def count_onehots(g):
                dve.wait_ge(s_cnt, g.n + 1)
                for j in range(TILES):
                    e = g.n * TILES + j
                    V.tensor_scalar(one_p[g.slot][:, j, :], iota_f[:, :], node_p[:, bass.ds(e, 1)],
                                    None, ALU.is_equal)
                    ins = V.tensor_scalar(one_b[g.slot][:, j, :], iota_f[:, 0:BLOCKS],
                                          node_b[:, bass.ds(e, 1)], None, ALU.is_equal)
                ins.then_inc(s_cntoh, 1)

            def clamp_filter(g1, g2):
                if g1:
                    dve.wait_ge(s_z2, g1.n + 1)
                    V.tensor_scalar(u2[g1.slot], ps_z2, CLAMP, None, ALU.min).then_inc(s_m2, 1)
                if g2:
                    dve.wait_ge(s_z1, g2.n + 1)
                    V.tensor_scalar(u1[g2.slot], ps_z1, be1[:, 0:1], CLAMP, ALU.add, ALU.min).then_inc(s_m1, 1)

            def finish_filter(g1, g2):
                if g1:
                    dve.wait_ge(s_l2, g1.n + 1)
                    V.scalar_tensor_tensor(filt[g1.slot], ps_z2, -LOG2, u2[g1.slot], ALU.add, ALU.max)\
                     .then_inc(s_f, 1)
                if g2:
                    dve.wait_ge(s_l1, g2.n + 1)
                    V.scalar_tensor_tensor(a1[g2.slot], ps_z1, be1[:, 1:2], u1[g2.slot], ALU.add, ALU.max)\
                     .then_inc(s_a1, 1)

            def messages(g):
                gathered(dve, 0, g)
                dve.wait_ge(s_f, g.n + 1)
                V.tensor_tensor(filt[g.slot], filt[g.slot], gath[g.slot], ALU.mult).then_inc(s_msg, 1)

            def fast_steps(L):
                def body(at):
                    prev, g = at(-1), at(0)
                    if L == 0:
                        clamp_filter(at(1), at(2))
                    if g:
                        dve.wait_ge(s_agg, L * G + g.n + 1)
                        dst_onehots(onehot[g.slot], dst_rel, g.n * TILES).then_inc(s_oh, 1)
                        if L == 1:
                            count_onehots(g)
                    if L == 0:
                        finish_filter(at(1), at(2))
                        if g:
                            messages(g)
                    if prev:
                        first = dve.value_load(base_i[0:1, bass.ds(prev.n, 1)], min_val=0, max_val=N - 1)
                        dve.wait_ge(s_agg, SLOTS + L * G + prev.n + 1)
                        dve.wait_ge(s_added, SLOTS + L * (G + 1) + prev.n + 1)
                        w = aggT[0:D, bass.ds(first, WINDOW)]
                        V.tensor_tensor(w, w, ps_agg[prev.slot], ALU.add).then_inc(s_added, 1)
                turns(dve, G, SLOTS, 2 if L == 0 else 0, 1, body)

            def general_steps(L):
                def body(at):
                    g = at(0)
                    if L == 0:
                        clamp_filter(at(1), at(2))
                        finish_filter(at(1), at(2))
                    if not g:
                        return
                    if L == 1:
                        count_onehots(g)
                    if L == 0:
                        messages(g)
                    done = (L * G + g.n) * NW
                    shifts = (L * G + g.n) * (NW + 1)
                    V.tensor_copy(wdst[:, :], dst_f[:, bass.ds(g.n * TILES, TILES)]).then_inc(s_gdst, 1)
                    with dve.Fori(0, NW) as w:
                        dve.wait_ge(s_gdst, shifts + w + 1)
                        dst_onehots(onehot[0], wdst, 0).then_inc(s_goh, 1)
                        dve.wait_ge(s_gsum, done + w + 1)
                        win = aggT[0:D, bass.ds(w * WINDOW, WINDOW)]
                        V.tensor_tensor(win, win, ps_agg[0], ALU.add).then_inc(s_gadd, 1)
                        V.tensor_scalar(wdst[:, :], wdst[:, :], -float(WINDOW), None, ALU.add).then_inc(s_gdst, 1)
                    dve.wait_ge(s_gadd, done + NW)
                    dve.wait_ge(s_gdst, shifts + NW + 1)
                turns(dve, G, SLOTS, 2 if L == 0 else 0, 0, body)
                dve.sem_inc(s_added, G)

            def aggregate(L):
                with dve.If(spilled > 0):
                    general_steps(L)
                with dve.Else():
                    fast_steps(L)
                dve.wait_ge(s_added, SLOTS + (L + 1) * (G + 1))
                dve.sem_inc(s_aggdone, 1)

            def clear_sums():
                V.memset(aggT[0:D, 0:N + WINDOW], 0.0).then_inc(s_added, 1)

            aggregate(0)

            def post0(at):
                p, c, n = at(-1), at(0), at(1)
                if n:
                    dve.wait_ge(s_pa, n.n + 1)
                    V.tensor_scalar(gcol[n.slot][0:D, :], ps[n.slot][0:D, 0:CN], bc[:, 0:1], CLAMP, ALU.add, ALU.min)\
                     .then_inc(s_pm, 1)
                if c:
                    dve.wait_ge(s_pl, c.n + 1)
                    dve.wait_ge(s_pb, c.n + 1)
                    V.scalar_tensor_tensor(col[c.slot][0:D, :], ps[c.slot][0:D, 0:CN], bc[:, 1:2],
                                           gcol[c.slot][0:D, :], ALU.add, ALU.max).then_inc(s_sp, 1)
                if p:
                    dve.wait_ge(s_pb, p.n + 3)
                    V.tensor_tensor(x_chunk(p.n), x_chunk(p.n), ps[2 + p.slot][0:P_NODE, 0:CF], ALU.add)\
                     .then_inc(s_px, 1)
            turns(dve, NC, 2, 1, 1, post0)
            clear_sums()
            make_table(1)
            aggregate(1)
            dve.wait_ge(s_cntall, 1)
            V.tensor_scalar(rq_v[0:P_NODE, 0:BLOCKS], ps_count, 1.0, None, ALU.max).then_inc(s_rqv, 1)
            rsqrt(P_NODE, BLOCKS, rs_deg[:, :])
            link(V.tensor_scalar(rc_deg[:, :], ps_count, 1.0, None, ALU.max))
            link(V.reciprocal(rc_deg[:, :], rc_deg[:, :]))
            link(V.tensor_scalar(to_spare, src_f[:, :], -1.0, spare[:, 0:1], ALU.mult, ALU.add))

            link(V.tensor_scalar(gin_eps[:, :], gin_eps[:, :], 1.0, None, ALU.add))
            dve.wait_ge(s_hT, 2 + NC)

            def combine(at):
                c, n = at(0), at(1)
                if n:
                    h = by_block(hT_chunk(n.n))
                    V.scalar_tensor_tensor(h, h, gin_eps[:, 0:1], agg_chunk(n.n), ALU.mult, ALU.add).then_inc(s_comb, 1)
                if c:
                    dve.wait_ge(s_h1, c.n + 1)
                    V.bn_stats(bn_raw[:, bass.ds(c.n, 1), :].rearrange("p o s -> p (o s)"), ps[c.slot][:, 0:CN])\
                     .then_inc(s_bn, 1)
            turns(dve, NC, 2, 1, 0, combine)
            dve.wait_ge(s_bn, 2 + NC)

            def batch_constants(rows, vec):
                t, sc = bn_t[0:rows, :], bn_sc[0:rows, :]
                link(V.bn_aggr(bn_mv[0:rows, :], bn_raw[0:rows, :, :].rearrange("p a b -> p (a b)")))
                V.tensor_scalar(rq_v[0:rows, 0:1], bn_mv[0:rows, 1:2], BN1_EPS, None, ALU.add).then_inc(s_rqv, 1)
                rsqrt(rows, 1, t)
                link(V.tensor_tensor(sc, t, vec[0:rows, 1:2], ALU.mult))
                link(V.tensor_tensor(t, bn_mv[0:rows, 0:1], vec[0:rows, 0:1], ALU.add))
                link(V.tensor_tensor(t, vec[0:rows, 0:1], t, ALU.subtract))
                link(V.tensor_tensor(t, t, sc, ALU.mult))
                V.tensor_tensor(bn_sh[0:rows, :], t, vec[0:rows, 2:3], ALU.add).then_inc(s_bnc, 1)
            batch_constants(P, gin_v1)

            def keep_second(at):
                c = at(0)
                dve.wait_ge(s_h2, c.n + 3)
                V.tensor_copy(hT_chunk(c.n), ps[2 + c.slot][0:D, 0:CN])
                V.bn_stats(bn_raw[0:D, bass.ds(c.n, 1), :].rearrange("p o s -> p (o s)"), ps[2 + c.slot][0:D, 0:CN])\
                 .then_inc(s_h2k, 1)
            turns(dve, NC, 2, 0, 0, keep_second)
            dve.wait_ge(s_h2k, 2 + NC)
            batch_constants(D, gin_v2)

            def post1(at):
                c = at(0)
                dve.wait_ge(s_yT, c.n + 3)
                V.tensor_tensor(x_chunk(c.n), x_chunk(c.n), ps[4 + c.slot][0:P_NODE, 0:CF], ALU.add)\
                 .then_inc(s_px, 1)
            turns(dve, NC, 2, 0, 0, post1)
            clear_sums()
            make_table(2)
            aggregate(2)
            dve.wait_ge(s_hT, 2 + 2 * NC)

            def post2(at):
                c, n = at(0), at(1)
                if n:
                    dve.wait_ge(s_pb, NC + n.n + 1)
                    V.tensor_tensor(by_block(hgcol[n.slot][0:D, :]), by_block(hT_chunk(n.n)), agg_chunk(n.n),
                                    ALU.mult).then_inc(s_hg, 1)
                if c:
                    own, nbr = ps[c.slot][0:P_NODE, 0:CF], ps[2 + c.slot][0:P_NODE, 0:CF]
                    t = hn[c.slot][:, :]
                    dve.wait_ge(s_pb, NC + c.n + 3)
                    V.tensor_tensor(by_block(t), by_block(nbr), spread(rs_deg[:, bass.ds(c.n * CB, CB)], D), ALU.mult)\
                     .then_inc(s_t1, 1)
                    dve.wait_ge(s_t1, c.n + 1)
                    V.tensor_tensor(t, t, own, ALU.add).then_inc(s_t2, 1)
                    dve.wait_ge(s_t2, c.n + 3)
                    V.scalar_tensor_tensor(t, t, LEAKY, t, ALU.mult, ALU.max).then_inc(s_t3, 1)
                    dve.wait_ge(s_t3, c.n + 1)
                    V.tensor_tensor(x_chunk(c.n), x_chunk(c.n), t, ALU.add).then_inc(s_px, 1)
            turns(dve, NC, 2, 1, 0, post2)
            link(V.tensor_scalar(dst_rel[:, :], src_f[:, :], 0.0, None, ALU.is_ge))
            link(V.tensor_tensor(to_spare, to_spare, dst_rel[:, :], ALU.mult))
            link(V.tensor_scalar(dst_rel[:, :], dst_rel[:, :], -1.0, 1.0, ALU.mult, ALU.add))
            link(V.tensor_scalar(dst_rel[:, :], dst_rel[:, :], spare1[:, 0:1], None, ALU.mult))
            link(V.tensor_tensor(dst_rel[:, :], dst_rel[:, :], src_f[:, :], ALU.add))
            make_table(3)

            src3 = dst_rel

            def total_steps(at):
                g, n = at(0), at(1)
                if n:
                    dve.wait_ge(s_same, n.n + 1)
                    for j in range(TILES):
                        ins = V.tensor_scalar(diag[n.slot][:, j * P:(j + 1) * P], ident[:, :],
                                              src3[:, bass.ds(n.n * TILES + j, 1)], None, ALU.mult)
                    ins.then_inc(s_diag, 1)
                if g:
                    dve.wait_ge(s_bsrc, g.n + 1)
                    dve.wait_ge(s_tot, g.n + 1)
                    for j in range(TILES):
                        tile = slice(j * P, (j + 1) * P)
                        ins = V.scalar_tensor_tensor(same[g.slot][:, tile], ps_src[g.slot][:, tile],
                                                     src3[:, bass.ds(g.n * TILES + j, 1)], upper[:, :],
                                                     ALU.is_equal, ALU.mult, accum_out=later[g.slot][:, j:j + 1])
                    ins.then_inc(s_same, 1)
                    dve.wait_ge(s_same, SLOTS + g.n + 1)
                    V.scalar_tensor_tensor(later[g.slot][:, :], later[g.slot][:, :], 1.5,
                                           to_spare[:, bass.ds(g.n * TILES, TILES)], ALU.is_gt, ALU.mult).then_inc(s_dup, 1)
                    gathered(dve, 3, g)
                    V.tensor_tensor(gath[g.slot].rearrange("p (j d) -> p j d", j=TILES),
                                    gath[g.slot].rearrange("p (j d) -> p j d", j=TILES),
                                    spread(w_edge[:, bass.ds(g.n * TILES, TILES)], D), ALU.mult).then_inc(s_wrow, 1)
                    dve.wait_ge(s_dup, g.n + 1)
                    wait_for(dve, s_scat[g.slot], 16 * TILES * g.round)
                    V.tensor_tensor(to_idx[g.slot][:, :], later[g.slot][:, :], src3[:, bass.ds(g.n * TILES, TILES)],
                                    ALU.add).then_inc(s_to, 1)
            turns(dve, G, SLOTS, 1, 0, total_steps, peel=1)
            for s in range(SLOTS):
                last = Item(0, G - 1 - (G - 1 - s) % SLOTS, SLOTS)
                dve.wait_ge(s_scat[s], 16 * TILES * (last.round + 1))
            dve.sem_inc(s_aggdone, 1)

            def post3(at):
                c, n = at(0), at(1)
                if n:
                    parts = part[n.slot]
                    dve.wait_ge(s_part[n.slot], 16 * TILES * (n.round + 1))
                    V.tensor_tensor(parts[0], parts[0], parts[1], ALU.add).then_inc(s_psum, 1)
                    V.tensor_tensor(parts[2], parts[2], parts[3], ALU.add).then_inc(s_psum, 1)
                    dve.wait_ge(s_psum, 3 * n.n + 2)
                    V.tensor_tensor(parts[0], parts[0], parts[2], ALU.add).then_inc(s_psum, 1)
                    dve.wait_ge(s_psum, 3 * n.n + 3)
                    wait_for(dve, s_pT, n.n - 1)
                    V.tensor_tensor(by_block(hn[n.slot][:, :]), by_block(parts[0]),
                                    spread(rc_deg[:, bass.ds(n.n * CB, CB)], D), ALU.mult).then_inc(s_pavg, 1)
                if c:
                    dve.wait_ge(s_pb, 2 * NC + c.n + 3)
                    V.scalar_tensor_tensor(x_chunk(c.n), ps[c.slot][0:P_NODE, 0:CF], 0.0, x_chunk(c.n),
                                           ALU.max, ALU.add).then_inc(s_px, 1)
            turns(dve, NC, 2, 1, 0, post3, peel=1)

        @block.tensor
        def _(pe):
            T = nc.tensor
            pe.wait_ge(s_ident, 2)
            for i in range(3 * GR):
                a, q = i // GR, i % GR
                r = min(P, G - q * P)
                if a < 2:
                    pe.wait_ge(s_rowf, i + 1)
                if i >= 2:
                    pe.wait_ge(s_list, i - 1)
                rows = row_float(a, q)[0:r, :].rearrange("g (e j) -> g j e", j=TILES)
                for j in range(TILES):
                    ins = T.transpose(ps[i % 2][:, j * P:j * P + r], rows[:, j, :], ident[0:r, 0:r])
                ins.then_inc(s_rowT, 1)
            pe.wait_ge(s_const, 1)
            pe.wait_ge(s_dstf, 1)
            T.matmul(ps[2][:, 0:G], ones_row[0:1, :], by_tile(dst_f[:, :])[0:1, :, 0], start=True, stop=True)\
             .then_inc(s_baseb, 1)
            pe.wait_ge(s_flags, 1)
            T.transpose(ps[3][0:1, 0:P], spill[:, 2:3], ident[:, :]).then_inc(s_flagT, 1)
            pe.wait_ge(s_fold, 1)
            for i in range(2):
                T.matmul(ps[4][0:D + 1, P * i:P * i + D], ones_row[0:1, 0:D + 1], fold[0:1, 2 * i, :],
                         start=True, stop=True)
                ins = T.matmul(ps[5][0:D + 1, P * i:P * i + D], last_row[0:1, :], fold[0:1, 2 * i + 1, :],
                               start=True, stop=True)
            ins.then_inc(s_foldb, 1)
            pe.wait_ge(s_ready, 1)

            def make_table(L):
                def body(at):
                    c = at(0)
                    n = L * NC + c.n
                    m = (L // 3) * NC + c.n
                    pe.wait_ge(s_hs, n + 3)
                    if L:
                        pe.wait_ge(s_hT, (L - 1) * NC + c.n + 1)
                    if L in (0, 3):
                        pe.wait_ge(s_col, m + 1)
                    pe.sem_inc(s_go, 1)
                    for j in range(CB):
                        ins = T.transpose(ps[c.slot][0:D, j * P_NODE:(j + 1) * P_NODE],
                                          hs[c.slot][:, j * D:(j + 1) * D], ident[0:P_NODE, 0:P_NODE])
                    ins.then_inc(s_tT, 1)
                    if L in (0, 3):
                        pe.wait_ge(s_col, m + 3)
                        pe.wait_ge(s_tab, n + 1)
                        for j in range(CB):
                            ins = T.matmul(ps[2 + c.slot][0:P_NODE, j * D:(j + 1) * D],
                                           col[c.slot][:, j * P_NODE:(j + 1) * P_NODE], (Wp if L else Wn)[:, :],
                                           start=True, stop=True)
                        ins.then_inc(s_proj, 1)
                turns(pe, NC, 2, 0, 0, body)
                pe.wait_ge(s_tab, 2 + (L + 1) * NC)
                if L:
                    pe.wait_ge(s_hT, 2 + L * NC)

            make_table(0)
            pe.wait_ge(s_spill, 1)
            spilled = pe.value_load(spill_i[0:1, 0:1], min_val=0, max_val=1)

            def filter_products(g1, g2, g3):
                if g1:
                    pe.wait_ge(s_a1, g1.n + 1)
                    wait_for(pe, s_f, g1.n)
                    T.matmul(ps_z2, ones_row[0:1, :], be2x[0:1, :], start=True, stop=False, skip_group_check=True)
                    for h in range(2):
                        ins = T.matmul(ps_z2[:, h * P:(h + 1) * P], a1[g1.slot][:, h * P:(h + 1) * P], We2[:, :],
                                       start=False, stop=(h == 1), skip_group_check=True)
                    ins.then_inc(s_z2, 1)
                if g3:
                    pe.wait_ge(s_ea[g3.slot], 16 * (g3.round + 1))
                    wait_for(pe, s_eTc, g3.n)
                    for h in range(2):
                        ins = T.transpose(ps_eT[:, h * P:(h + 1) * P], eat[g3.slot][:, h * P:(h + 1) * P], ident[:, :])
                    ins.then_inc(s_eT, 1)
                if g2:
                    pe.wait_ge(s_eTc, g2.n + 1)
                    wait_for(pe, s_a1, g2.n)
                    T.matmul(ps_z1, We1[:, :], eaT[g2.slot], start=True, stop=True).then_inc(s_z1, 1)

            def rows_ready(L, g):
                if L == 0:
                    pe.wait_ge(s_msg, SLOTS + g.n + 1)
                else:
                    gathered(pe, L, g)

            def sum_window(L, g, slot):
                rows = filt[g.slot] if L == 0 else gath[g.slot]
                for j in range(TILES):
                    ins = T.matmul(ps_agg[slot], rows[:, j * D:(j + 1) * D], onehot[slot][:, j * WINDOW:(j + 1) * WINDOW],
                                   start=(j == 0), stop=(j == TILES - 1))
                return ins

            def count_step(g):
                pe.wait_ge(s_cntoh, g.n + 1)
                for j in range(TILES):
                    ins = T.matmul(ps_count, one_p[g.slot][:, j, 0:P_NODE], one_b[g.slot][:, j, :],
                                   start=False, stop=False, skip_group_check=True)
                ins.then_inc(s_cnt, 1)

            def fast_steps(L):
                def body(at):
                    g = at(0)
                    if L == 0:
                        filter_products(at(1), at(2), at(3))
                    if not g:
                        return
                    if L == 1:
                        count_step(g)
                    rows_ready(L, g)
                    pe.wait_ge(s_oh, L * G + g.n + 1)
                    pe.wait_ge(s_added, L * (G + 1) + g.n + 2)
                    sum_window(L, g, g.slot).then_inc(s_agg, 1)
                turns(pe, G, SLOTS, 3 if L == 0 else 0, 0, body)

            def general_steps(L):
                def body(at):
                    g = at(0)
                    if L == 0:
                        filter_products(at(1), at(2), at(3))
                    if not g:
                        return
                    if L == 1:
                        count_step(g)
                    rows_ready(L, g)
                    done = (L * G + g.n) * NW
                    pe.sem_inc(s_go, 1)
                    with pe.Fori(0, NW) as w:
                        pe.wait_ge(s_goh, done + w + 1)
                        rows = filt[g.slot] if L == 0 else gath[g.slot]
                        for j in range(TILES):
                            ins = T.matmul(ps_agg[0], rows[:, j * D:(j + 1) * D],
                                           onehot[0][:, j * WINDOW:(j + 1) * WINDOW],
                                           start=(j == 0), stop=(j == TILES - 1))
                        ins.then_inc(s_gsum, 1)
                    pe.drain().then_inc(s_agg, 1)
                turns(pe, G, SLOTS, 3 if L == 0 else 0, 0, body)

            def aggregate(L):
                if L == 1:
                    T.matmul(ps_count, zero_row[0:1, 0:P_NODE], zero_row[0:1, 0:BLOCKS], start=True, stop=False,
                             skip_group_check=True)
                with pe.If(spilled > 0):
                    general_steps(L)
                with pe.Else():
                    fast_steps(L)
                if L == 1:
                    T.matmul(ps_count, zero_row[0:1, 0:P_NODE], zero_row[0:1, 0:BLOCKS], start=False, stop=True,
                             skip_group_check=True).then_inc(s_cntall, 1)
                pe.wait_ge(s_aggdone, L + 1)

            aggregate(0)

            def post0(at):
                c, n = at(0), at(1)
                if n:
                    pe.wait_ge(s_sp, n.n + 1)
                    T.matmul(ps[n.slot][:, 0:CN], Wc[:, :], agg_chunk(n.n), start=True, stop=True).then_inc(s_pa, 1)
                if c:
                    pe.wait_ge(s_sp, c.n + 3)
                    pe.wait_ge(s_px, c.n + 1)
                    for j in range(CB):
                        ins = T.matmul(ps[2 + c.slot][0:P_NODE, j * D:(j + 1) * D],
                                       col[c.slot][:, j * P_NODE:(j + 1) * P_NODE], Wo[:, :], start=True, stop=True)
                    ins.then_inc(s_pb, 1)
            turns(pe, NC, 2, 1, 0, post0)
            make_table(1)
            aggregate(1)

            def hidden(at):
                c = at(0)
                pe.wait_ge(s_comb, c.n + 1)
                pe.wait_ge(s_bn, c.n + 1)
                T.matmul(ps[c.slot][:, 0:CN], gin_W1[:, :], hT_chunk(c.n), start=True, stop=True).then_inc(s_h1, 1)
            turns(pe, NC, 2, 0, 0, hidden)
            pe.wait_ge(s_bnc, 1)

            def second(at):
                c, n = at(0), at(1)
                if n:
                    pe.wait_ge(s_act1, n.n + 1)
                    T.matmul(ps[n.slot][:, 0:CN], gin_W1[:, :], hT_chunk(n.n), start=True, stop=True).then_inc(s_h1b, 1)
                if c:
                    pe.wait_ge(s_act1, c.n + 3)
                    pe.wait_ge(s_h2k, c.n + 1)
                    T.matmul(ps[2 + c.slot][0:D, 0:CN], gin_W2[:, :], gcol[c.slot][:, :], start=True, stop=True)\
                     .then_inc(s_h2, 1)
            turns(pe, NC, 2, 1, 0, second)

            def gin_output(at):
                c = at(0)
                pe.wait_ge(s_y, c.n + 1)
                pe.wait_ge(s_px, NC + c.n + 1)
                pe.sem_inc(s_go, 1)
                for j in range(CB):
                    ins = T.transpose(ps[4 + c.slot][0:P_NODE, j * D:(j + 1) * D],
                                      col[c.slot][0:D, j * P_NODE:(j + 1) * P_NODE], ident[0:D, 0:D])
                ins.then_inc(s_yT, 1)
            turns(pe, NC, 2, 0, 0, gin_output)
            make_table(2)
            aggregate(2)

            def products(at):
                c = at(0)
                own, nbr = ps[c.slot], ps[2 + c.slot]
                pe.wait_ge(s_stg, c.n + 1)
                pe.wait_ge(s_hg, c.n + 1)
                pe.wait_ge(s_t2, c.n + 1)
                for j in range(CB):
                    nodes, out = slice(j * P_NODE, (j + 1) * P_NODE), slice(j * D, (j + 1) * D)
                    T.matmul(own[0:P_NODE, out], col[c.slot][0:D, nodes], bi_W1[:, :], start=True, stop=True)
                    T.matmul(nbr[0:P_NODE, out], gcol[c.slot][0:D, nodes], bi_W1[:, :], start=True, stop=False)
                    ins = T.matmul(nbr[0:P_NODE, out], hgcol[c.slot][0:D, nodes], bi_W2[:, :],
                                   start=False, stop=True)
                ins.then_inc(s_pb, 1)
            turns(pe, NC, 2, 0, 0, products)
            make_table(3)

            def total_steps(at):
                g, n = at(0), at(1)
                if n:
                    pe.wait_ge(s_diag, n.n + 1)
                    pe.wait_ge(s_same, n.n + 1)
                    T.matmul(ps_src[n.slot][:, :], ones_pp[:, :], diag[n.slot][:, :], start=True, stop=True)\
                     .then_inc(s_bsrc, 1)
                if g:
                    pe.wait_ge(s_same, SLOTS + g.n + 1)
                    pe.wait_ge(s_wrow, g.n + 1)
                    pe.wait_ge(s_totc, g.n + 1)
                    for j in range(TILES):
                        ins = T.matmul(ps_total[g.slot][:, j * D:(j + 1) * D], same[g.slot][:, j * P:(j + 1) * P],
                                       gath[g.slot][:, j * D:(j + 1) * D], start=True, stop=True)
                    ins.then_inc(s_tot, 1)
            turns(pe, G, SLOTS, 1, 0, total_steps)

            def update(at):
                c, n = at(0), at(1)
                if n:
                    pe.wait_ge(s_pavg, n.n + 3)
                    wait_for(pe, s_pTc, n.n - 1)
                    pe.sem_inc(s_go, 1)
                    for j in range(CB):
                        ins = T.transpose(ps[4 + n.slot][0:D, j * P_NODE:(j + 1) * P_NODE],
                                          hn[n.slot][:, j * D:(j + 1) * D], ident[0:P_NODE, 0:P_NODE])
                    ins.then_inc(s_pT, 1)
                if c:
                    pe.wait_ge(s_stg, NC + c.n + 1)
                    pe.wait_ge(s_pTc, c.n + 1)
                    pe.wait_ge(s_px, 3 * NC + c.n + 1)
                    for j in range(CB):
                        nodes, out = slice(j * P_NODE, (j + 1) * P_NODE), slice(j * D, (j + 1) * D)
                        T.matmul(ps[c.slot][0:P_NODE, out], col[c.slot][:, nodes], Wu[:, :], start=True, stop=False)
                        ins = T.matmul(ps[c.slot][0:P_NODE, out], gcol[c.slot][0:D, nodes], Wu_agg[:, :],
                                       start=False, stop=True)
                    ins.then_inc(s_pb, 1)
            turns(pe, NC, 2, 1, 0, update, peel=1)


INPUTS = ["x", "src", "dst", "edge_attr_64", "edge_weight", "L0_gnn_We1", "L0_gnn_be1", "L0_gnn_We2", "L0_gnn_be2",
          "L0_gnn_Wn", "L0_gnn_bn", "L0_gnn_Wc", "L0_gnn_bc", "L0_gnn_Wo", "L0_gnn_bo", "L1_gnn_epsilon", "L1_gnn_W1",
          "L1_gnn_b1", "L1_gnn_g1", "L1_gnn_be1", "L1_gnn_W2", "L1_gnn_b2", "L1_gnn_g2", "L1_gnn_be2", "L2_gnn_W1",
          "L2_gnn_W2", "L3_gnn_W_prep", "L3_gnn_b_prep", "L3_gnn_gamma_p", "L3_gnn_beta_p", "L3_gnn_mean_p",
          "L3_gnn_var_p", "L3_gnn_W_upd", "L3_gnn_b_upd", "L3_gnn_gamma_u", "L3_gnn_beta_u", "L3_gnn_mean_u",
          "L3_gnn_var_u"]


def kernel(**inputs):
    import numpy as np
    import concourse.bacc as bacc
    from concourse import mybir as my
    from concourse.bass_utils import run_bass_kernel_spmd

    nc = bacc.Bacc("TRN2", target_bir_lowering=False, num_devices=1)
    arrays, io = {}, {}
    for name in INPUTS:
        a = np.ascontiguousarray(inputs[name])
        if name == "L1_gnn_epsilon":
            a = a.reshape(1, 1)
        arrays[f"in_{name}"] = a
        io[name] = nc.dram_tensor(f"in_{name}", a.shape, my.dt.from_np(a.dtype), kind="ExternalInput").ap()
    shape = inputs["x"].shape
    io["out"] = nc.dram_tensor("out_x", shape, my.dt.float32, kind="ExternalOutput").ap()
    rows = shape[0] + SPARE
    acc = [nc.dram_tensor(f"acc{j}", (rows, shape[1]), my.dt.float32, kind="Internal").ap() for j in range(4)]
    table = [nc.dram_tensor(f"table{L}", shape, my.dt.float32, kind="Internal").ap() for L in range(4)]
    gnn_layers(nc, io, table, acc)
    r = run_bass_kernel_spmd(nc, [arrays], core_ids=[0])
    return r.results[0]["out_x"]
```

```python
import concourse.bass as bass
from concourse import mybir
from contextlib import ExitStack

FP32 = mybir.dt.float32
BF16 = mybir.dt.bfloat16
I32 = mybir.dt.int32
ALU = mybir.AluOpType
ACT = mybir.ActivationFunctionType
AX = mybir.AxisListType

D = 64
P = 128
P_NODE = 125
TILES = 4
STEP = TILES * P
SLOTS = 3
WINDOW = 128
CB = 4
CN = CB * P_NODE
CF = CB * D
LOG2 = 0.6931471805599453
CLAMP = 30.0
LN_EPS = 1e-5
BN1_EPS = 1e-5
BN3_EPS = 1e-3
LEAKY = 0.01
SPARE = CN


class Item:

    def __init__(self, rnd, off, unroll):
        self.slot = off % unroll
        self.round = rnd + off // unroll
        self.n = rnd * unroll + off


def turns(eng, count, unroll, lead, lag, body, peel=0):

    def fixed(t):
        return lambda o: Item(0, t + o, unroll) if 0 <= t + o < count else None

    first = max(-(-lag // unroll), peel)
    last = (count - lead) // unroll
    if last - first < 1:
        for t in range(-lead, count + lag):
            body(fixed(t))
        return
    for t in range(-lead, first * unroll):
        body(fixed(t))
    with eng.Fori(first, last) as rnd:
        for s in range(unroll):
            body(lambda o, s=s: Item(rnd, s + o, unroll))
    for t in range(last * unroll, count + lag):
        body(fixed(t))


def gnn_layers(nc, io, table, acc):
    N = io["x"].shape[0]
    E = io["src"].shape[0]
    BLOCKS = N // P_NODE
    NC = BLOCKS // CB
    G = -(-E // STEP)
    TAIL = E - (G - 1) * STEP
    NW = -(-N // WINDOW)
    GR = -(-G // P)
    assert N % CN == 0 and G % SLOTS == 1 and TAIL % TILES == 0 and G <= 512 and BLOCKS <= 512 and G > SLOTS

    ctx = ExitStack()
    with ctx:
        def sb(name, shape, dt=FP32):
            return ctx.enter_context(nc.sbuf_tensor(name, shape, dt))

        def bank(name, shape, dt=FP32):
            return ctx.enter_context(nc.psum_tensor(name, shape, dt))

        def sem(name):
            return ctx.enter_context(nc.semaphore(name))

        ZF = 4 * D
        x_nm = sb("x_nm", [P_NODE, BLOCKS * D])
        aggT = sb("aggT", [P, max(N + WINDOW, GR * 3 * STEP, 12 * TILES * P)])
        SHARED = 6 * SLOTS * TILES * D
        hT = sb("hT", [P, max(N, SHARED, GR * 3 * STEP)])
        src_f = sb("src_f", [P, G * TILES])
        dst_rel = sb("dst_rel", [P, G * TILES])
        w_edge = sb("w_edge", [P, G * TILES])
        node_pb = sb("node_pb", [P, 2 * G * TILES], BF16)
        node_p, node_b = node_pb[:, 0:G * TILES], node_pb[:, G * TILES:2 * G * TILES]
        to_spare = node_pb[:, :].bitcast(FP32)
        dst_f = sb("dst_f", [P, G * TILES])
        base_i = sb("base_i", [1, G], I32)
        upper = sb("upper", [P, P])
        zeros = sb("zeros", [P_NODE, ZF])
        spare = sb("spare", [P, 1])
        spare1 = sb("spare1", [P, 1])
        spare_i = sb("spare_i", [P, 1], I32)
        ident = sb("ident", [P, P])
        iota_f = sb("iota_f", [P, WINDOW])
        ones_row = sb("ones_row", [1, P])
        zero_row = sb("zero_row", [1, P], BF16)
        last_row = sb("last_row", [1, D + 1])
        half = sb("half", [P, 1])
        spill = sb("spill", [P, 8])
        spill_i = sb("spill_i", [1, 1], I32)
        stats = sb("stats", [P_NODE, BLOCKS, 6])
        mean = sb("mean", [P_NODE, BLOCKS])
        rstd = sb("rstd", [P_NODE, BLOCKS])
        rs_deg = sb("rs_deg", [P_NODE, BLOCKS])
        rc_deg = sb("rc_deg", [P_NODE, BLOCKS])
        rq_v = sb("rq_v", [P, max(BLOCKS, D)])
        rq_l = sb("rq_l", [P, max(BLOCKS, D)])
        rq_y = sb("rq_y", [P, max(BLOCKS, D)])
        rq_t = sb("rq_t", [P, max(BLOCKS, D)])
        bn_raw = sb("bn_raw", [P, NC, 6])
        bn_mv = sb("bn_mv", [P, 2])
        bn_sc = sb("bn_sc", [P, 1])
        bn_sh = sb("bn_sh", [P, 1])
        bn_t = sb("bn_t", [P, 1])
        bn_up = sb("bn_up", [P, 2])

        We1 = sb("We1", [P, P])
        We2 = sb("We2", [P, P])
        be2x = sb("be2x", [1, 4 * D])
        be2b = sb("be2b", [P, 4 * D])
        be1 = sb("be1", [P, 2])
        Wn = sb("Wn", [D + 1, D])
        Wc = sb("Wc", [D, P])
        bc = sb("bc", [D, 2])
        Wo = sb("Wo", [D + 1, D])
        gin_W1 = sb("gin_W1", [D, P])
        gin_W2 = sb("gin_W2", [P, D])
        gin_v1 = sb("gin_v1", [P, 3])
        gin_v2 = sb("gin_v2", [D, 3])
        gin_eps = sb("gin_eps", [D, 1])
        bi_W = sb("bi_W", [2 * D, D])
        Wp = sb("Wp", [D + 1, D])
        Wu = sb("Wu", [2 * D, D])
        bu = sb("bu", [1, 4, D])
        bu_b = sb("bu_b", [P, 4 * D])
        rows3 = sb("rows3", [1, 8, D])
        fold = sb("fold", [1, 4, D])

        gath_all = sb("gath", [P, SLOTS * TILES * D])
        gath = [gath_all[:, s * TILES * D:(s + 1) * TILES * D] for s in range(SLOTS)]
        idx = [sb(f"idx{s}", [P, TILES], I32) for s in range(SLOTS)]
        onehot = [sb(f"onehot{s}", [P, TILES * WINDOW]) for s in range(SLOTS)]
        one_p = [sb(f"one_p{s}", [P, TILES, P], BF16) for s in range(SLOTS)]
        one_b = [sb(f"one_b{s}", [P, TILES, BLOCKS], BF16) for s in range(SLOTS)]
        wdst = sb("wdst", [P, TILES])

        def shared(kind, s):
            o = (kind * SLOTS + s) * TILES * D
            return hT[:, o:o + TILES * D]

        eat = [shared(0, s) for s in range(SLOTS)]
        eaT = [shared(1, s) for s in range(SLOTS)]
        u1 = [shared(2, s) for s in range(SLOTS)]
        a1 = [shared(3, s) for s in range(SLOTS)]
        u2 = [shared(4, s) for s in range(SLOTS)]
        filt = [shared(5, s) for s in range(SLOTS)]

        hn = [sb(f"hn{k}", [P_NODE, CF]) for k in range(2)]
        hs = [sb(f"hs{k}", [P_NODE, CF]) for k in range(2)]
        tab = [sb(f"tab{k}", [P_NODE, CF]) for k in range(2)]
        col = [sb(f"col{k}", [D + 1, CN]) for k in range(2)]
        gcol = [onehot[k][:, 0:CN] for k in range(2)]

        def in_agg(kind, s):
            o = (kind * SLOTS + s) * TILES * P
            return aggT[:, o:o + TILES * P]

        same = [in_agg(0, s) for s in range(SLOTS)]
        total = [in_agg(1, s)[:, 0:TILES * D] for s in range(SLOTS)]
        srcs = [in_agg(1, s)[:, TILES * D:TILES * D + TILES] for s in range(SLOTS)]
        from_win = [in_agg(2, s) for s in range(SLOTS)]
        win = [in_agg(3, s)[:, 0:D] for s in range(SLOTS)]
        later = [sb(f"later{s}", [P, TILES]) for s in range(SLOTS)]
        to_idx = [sb(f"to_idx{s}", [P, TILES], I32) for s in range(SLOTS)]
        part = [[in_agg(2, k)[0:P_NODE, 0:CF], in_agg(2, k)[0:P_NODE, CF:2 * CF],
                 in_agg(3, k)[0:P_NODE, 0:CF], in_agg(3, k)[0:P_NODE, CF:2 * CF]] for k in range(2)]

        def row_view(a, q):
            o = (a * GR + q) * STEP
            return aggT[:, o:o + STEP] if a == 2 else aggT[:, o:o + STEP].bitcast(I32)

        def row_float(a, q):
            o = (a * GR + q) * STEP
            return aggT[:, o:o + STEP] if a == 2 else hT[:, o:o + STEP]

        base_f = hT[0:1, 2 * G * TILES:2 * G * TILES + G]
        iota_i = gath_all[:, 0:WINDOW].bitcast(I32)
        sp_q = hT[:, G * TILES:2 * G * TILES]
        sp_r = aggT[:, 0:G * TILES]
        sp_t = aggT[:, G * TILES:2 * G * TILES]
        sp_i = aggT[:, 2 * G * TILES:3 * G * TILES].bitcast(I32)

        ps = [bank(f"ps{i}", [P, 512]) for i in range(8)]
        ps_eT, ps_z2 = ps[0][:, 0:256], ps[2][:, 0:256]
        ps_z1 = [ps[b][:, 0:256] for b in (1, 6, 7)]
        ps_agg = [ps[3 + s][0:D, 0:WINDOW] for s in range(SLOTS)]
        ps_count = ps[6][0:P_NODE, 0:BLOCKS]
        ps_src = [ps[s] for s in range(SLOTS)]
        ps_from = [ps[3 + s] for s in range(SLOTS)]
        ps_total = ps[6][:, 0:TILES * D]

        s_x = sem("x_loaded")
        s_w = sem("weights_loaded")
        s_rows = sem("edge_rows_loaded")
        s_pad = sem("padding_written")
        s_iota = sem("iota_written")
        s_zero = sem("weights_zeroed")
        s_const = sem("constants_written")
        s_ident = sem("identity_written")
        s_rowf = sem("edge_rows_as_float")
        s_rowT = sem("edge_rows_transposed")
        s_list = sem("edge_lists_written")
        s_setup = sem("vector_setup_step")
        s_pstep = sem("gpsimd_step")
        s_lists3 = sem("layer3_lists_ready")
        s_dstf = sem("dst_as_float")
        s_baseb = sem("bases_broadcast")
        s_flags = sem("spill_flags_written")
        s_flagT = sem("spill_flags_transposed")
        s_spill = sem("spill_flag_ready")
        s_rqv = sem("rsqrt_argument_ready")
        s_rqy = sem("rsqrt_guess_ready")
        s_rqn = sem("rsqrt_newton_step")
        s_fold = sem("bn_fold_rows_ready")
        s_foldb = sem("bn_fold_broadcast")
        s_ready = sem("weights_ready")
        s_stat = sem("layernorm_stats")
        s_hn = sem("normalised_chunk")
        s_hs = sem("relu_chunk")
        s_tT = sem("chunk_transposed")
        s_hT = sem("feature_major_kept")
        s_col = sem("feature_major_staged")
        s_proj = sem("table_projected")
        s_tab = sem("table_chunk_ready")
        s_tdma = [sem(f"table_chunk_stored{k}") for k in range(2)]
        s_idx = sem("indices_staged")
        s_gath = [[sem(f"rows_gathered_L{L}_{s}") for s in range(SLOTS)] for L in range(4)]
        s_go = sem("waits_carried")
        s_ea = [sem(f"edge_attr_loaded{s}") for s in range(SLOTS)]
        s_eT = sem("edge_attr_transposed")
        s_eTc = sem("edge_attr_T_copied")
        s_z1 = sem("z1_ready")
        s_m1 = sem("z1_clamped")
        s_e1 = sem("exp1_done")
        s_l1 = sem("log1_done")
        s_a1 = sem("a1_ready")
        s_z2 = sem("z2_ready")
        s_zb = sem("z2_with_bias")
        s_m2 = sem("z2_magnitude")
        s_e2 = sem("exp2_done")
        s_l2 = sem("log2_done")
        s_f = sem("filter_ready")
        s_msg = sem("messages_ready")
        s_oh = sem("onehot_ready")
        s_agg = sem("window_summed")
        s_added = sem("window_added")
        s_cntoh = sem("count_onehots_ready")
        s_cnt = sem("count_step_summed")
        s_cntall = sem("count_complete")
        s_goh = sem("general_onehot_ready")
        s_gsum = sem("general_window_summed")
        s_gadd = sem("general_window_added")
        s_gdst = sem("general_dst_shifted")
        s_aggdone = sem("layer_aggregated")
        s_zeroed = sem("accumulators_zeroed")
        s_srcs = sem("src_staged")
        s_win = [sem(f"table_window_loaded{s}") for s in range(SLOTS)]
        s_ohw = sem("weighted_onehots_ready")
        s_from = sem("window_to_totals_matrix")
        s_fromc = sem("window_to_totals_copied")
        s_bsrc = sem("src_broadcast")
        s_same = sem("same_src_ready")
        s_dup = sem("duplicates_redirected")
        s_to = sem("scatter_rows_ready")
        s_wrow = sem("weighted_rows_ready")
        s_tot = sem("row_totals_summed")
        s_totc = sem("row_totals_copied")
        s_scat = [sem(f"rows_scattered_tile{j}") for j in range(TILES)]
        s_part = [sem(f"accumulators_loaded{k}") for k in range(2)]
        s_psum = sem("accumulators_added")
        s_pavg = sem("average_ready")
        s_pT = sem("average_transposed")
        s_pTc = sem("average_staged")
        s_ub = sem("update_with_bias")
        s_pa = sem("conv_product_ready")
        s_pm = sem("conv_clamped")
        s_pe = sem("conv_exp")
        s_pl = sem("conv_log")
        s_sp = sem("conv_softplus")
        s_pb = sem("layer_products_ready")
        s_px = sem("residual_added")
        s_comb = sem("combined_ready")
        s_h1 = sem("gin_hidden_product")
        s_bn = sem("batchnorm_stats")
        s_bnc = sem("batchnorm_constants")
        s_hk = sem("gin_hidden_kept")
        s_act1 = sem("gin_hidden_activated")
        s_h2 = sem("gin_second_product")
        s_h2k = sem("gin_second_kept")
        s_y = sem("gin_output_scaled")
        s_yT = sem("gin_output_transposed")
        s_stg = sem("operands_staged")
        s_hg = sem("h_times_sum")
        s_t1 = sem("neighbour_term_scaled")
        s_t2 = sem("terms_summed")
        s_t3 = sem("leaky_relu_done")
        s_out = sem("output_stored")

        block = ctx.enter_context(nc.Block())

        def hidden_chunk(half, c):
            return (aggT if half else hT)[D:2 * D, bass.ds(c * CN, CN)]

        def agg_chunk(c):
            return aggT[0:D, 0:N].rearrange("k (p b) -> k b p", b=BLOCKS)[:, bass.ds(c * CB, CB), :]

        def hT_chunk(c):
            return hT[0:D, bass.ds(c * CN, CN)]

        def x_chunk(c):
            return x_nm[:, bass.ds(c * CF, CF)]

        def by_block(ap):
            return ap.rearrange("k (a b) -> k a b", a=CB)

        def by_tile(ap):
            return ap.rearrange("p (g j) -> p g j", j=TILES)

        def spread(ap, n):
            return ap.rearrange("p (a o) -> p a o", o=1).to_broadcast([ap.shape[0], ap.shape[1], n])

        def table_uses(k, L, rnd=0):
            return L * ((NC + 1 - k) // 2) + rnd

        def gathered(eng, L, g):
            eng.wait_ge(s_gath[L][g.slot], 16 * TILES * (g.round + 1))

        def wait_for(eng, s, n):
            if not (isinstance(n, int) and n <= 0):
                eng.wait_ge(s, n)

        def scattered(eng, n):
            for j in range(TILES):
                wait_for(eng, s_scat[j], 16 * n)

        @block.sync
        def _(sp):
            xd = io["x"].rearrange("(p b) d -> p (b d)", b=BLOCKS)
            sp.dma_start(x_nm[0:112, :], xd[0:112, :]).then_inc(s_x, 16)
            sp.dma_start(x_nm[112:P_NODE, :], xd[112:P_NODE, :]).then_inc(s_x, 16)
            sp.wait_ge(s_pad, 3)
            for a, name in enumerate(("src", "dst", "edge_weight")):
                for q in range(GR):
                    rows = min(P, G - 1 - q * P)
                    if rows > 0:
                        sp.dma_start(row_view(a, q)[0:rows, :],
                                     io[name][q * P * STEP:(q * P + rows) * STEP].rearrange("(g e) -> g e", e=STEP))\
                          .then_inc(s_rows, 16)
                r = (G - 1) % P
                sp.dma_start(row_view(a, GR - 1)[r:r + 1, 0:TAIL],
                             io[name][(G - 1) * STEP:E].rearrange("(o e) -> o e", o=1)).then_inc(s_rows, 16)

            def store_table(L):
                to = table[L].rearrange("(p b) d -> p (b d)", b=BLOCKS)

                def body(at):
                    c = at(0)
                    sp.wait_ge(s_tab, L * NC + c.n + 3)
                    sp.dma_start(to[:, bass.ds(c.n * CF, CF)], tab[c.slot][:, :]).then_inc(s_tdma[c.slot], 16)
                turns(sp, NC, 2, 0, 0, body)

            store_table(0)
            ea = io["edge_attr_64"]
            rows = ea[0:(G - 1) * STEP, :].rearrange("(r j) d -> r (j d)", j=TILES)
            sp.wait_ge(s_added, SLOTS + 1)

            def load_attr(at):
                g = at(0)
                sp.wait_ge(s_eT, g.n + 1)
                sp.dma_start(eat[g.slot], rows[bass.ds(g.n * P, P), :]).then_inc(s_ea[g.slot], 16)
            turns(sp, G - 1, SLOTS, 0, 0, load_attr)
            last = Item(0, G - 1, SLOTS)
            sp.wait_ge(s_eT, last.n + 1)
            sp.dma_start(eat[last.slot][0:TAIL // TILES, :],
                         ea[(G - 1) * STEP:E, :].rearrange("(r j) d -> r (j d)", j=TILES)).then_inc(s_ea[last.slot], 16)
            sp.wait_ge(s_zero, 1)
            for j in range(TILES):
                to = acc[j].rearrange("(n p b) d -> n p (b d)", p=P_NODE, b=4)

                def store_zeros(at, to=to):
                    z = at(0)
                    sp.dma_start(to[bass.ds(z.n, 1), :, :].rearrange("o p f -> (o p) f"), zeros[:, :])\
                      .then_inc(s_zeroed, 16)
                turns(sp, (N + SPARE) // (4 * P_NODE), 1, 0, 0, store_zeros)
            for L in (1, 2, 3):
                store_table(L)
            sp.wait_ge(s_spill, 1)
            with sp.If(sp.value_load(spill_i[0:1, 0:1], min_val=0, max_val=1) < 1):
                for k in range(2):
                    sp.wait_ge(s_tdma[k], 16 * table_uses(k, 4))

                def load_window(at):
                    g = at(0)
                    first = sp.value_load(base_i[0:1, bass.ds(g.n, 1)], min_val=0, max_val=N - WINDOW)
                    sp.wait_ge(s_tot, g.n + 1)
                    sp.dma_start(win[g.slot], table[3][bass.ds(first, WINDOW), :]).then_inc(s_win[g.slot], 16)
                turns(sp, G, SLOTS, 0, 0, load_window)
            sp.wait_ge(s_aggdone, 4)
            views = [acc[j][0:N, :].rearrange("(p b) d -> p (b d)", b=BLOCKS) for j in range(TILES)]

            def load_parts(at):
                c = at(0)
                sp.wait_ge(s_pavg, c.n + 1)
                for j in range(TILES):
                    sp.dma_start(part[c.slot][j], views[j][:, bass.ds(c.n * CF, CF)]).then_inc(s_part[c.slot], 16)
            turns(sp, NC, 2, 0, 0, load_parts)
            sp.wait_ge(s_px, 2 + 4 * NC)
            od = io["out"].rearrange("(p b) d -> p (b d)", b=BLOCKS)
            sp.dma_start(od[0:112, :], x_nm[0:112, :]).then_inc(s_out, 16)
            sp.dma_start(od[112:P_NODE, :], x_nm[112:P_NODE, :]).then_inc(s_out, 16)
            sp.wait_ge(s_out, 32)

        @block.gpsimd
        def _(pool):
            psteps = [0]

            def plink(ins):
                psteps[0] += 1
                ins.then_inc(s_pstep, 1)
                pool.wait_ge(s_pstep, psteps[0])

            for a in range(2):
                nc.gpsimd.memset(row_view(a, GR - 1), -1).then_inc(s_pad, 1)
            nc.gpsimd.memset(row_view(2, GR - 1), 0.0).then_inc(s_pad, 1)
            nc.gpsimd.iota(iota_i, [[1, WINDOW]], base=0, channel_multiplier=0).then_inc(s_iota, 1)
            nc.gpsimd.memset(ident[:, :], 0.0).then_inc(s_ident, 1)
            pool.wait_ge(s_ident, 1)
            nc.gpsimd.affine_select(out=ident[:, :], in_=ident[:, :], compare_op=ALU.not_equal, fill=1.0,
                                    base=0, pattern=[[-1, P]], channel_multiplier=1).then_inc(s_ident, 1)
            nc.gpsimd.memset(upper[:, :], 1.0).then_inc(s_ident, 1)
            nc.gpsimd.iota(spare_i[:, :], [[0, 1]], base=N, channel_multiplier=1).then_inc(s_iota, 1)
            pool.wait_ge(s_ident, 3)
            nc.gpsimd.affine_select(out=upper[:, :], in_=upper[:, :], compare_op=ALU.is_ge, fill=0.0,
                                    base=0, pattern=[[1, P]], channel_multiplier=-1).then_inc(s_ident, 1)
            pool.wait_ge(s_rows, 16 * 3 * (-(-(G - 1) // P) + 1))
            for a in range(2):
                for q in range(GR):
                    r = min(P, G - q * P)
                    nc.gpsimd.tensor_copy(row_float(a, q)[0:r, :], row_view(a, q)[0:r, :]).then_inc(s_rowf, 1)
            pool.wait_ge(s_spill, 1)
            gp = nc.gpsimd
            plink(gp.tensor_scalar(sp_i, src_f[:, :], 1.0 / BLOCKS, None, ALU.mult))
            plink(gp.tensor_copy(sp_q, sp_i))
            plink(gp.tensor_scalar(sp_r, sp_q, -float(BLOCKS), None, ALU.mult))
            plink(gp.tensor_tensor(sp_r, sp_r, src_f[:, :], ALU.add))
            plink(gp.tensor_scalar(sp_t, sp_r, 0.0, None, ALU.is_lt))
            plink(gp.tensor_tensor(sp_q, sp_q, sp_t, ALU.subtract))
            plink(gp.tensor_scalar(sp_t, sp_t, float(BLOCKS), None, ALU.mult))
            plink(gp.tensor_tensor(sp_r, sp_r, sp_t, ALU.add))
            plink(gp.tensor_scalar(sp_t, sp_r, float(BLOCKS), None, ALU.is_ge))
            plink(gp.tensor_tensor(node_p, sp_q, sp_t, ALU.add))
            plink(gp.tensor_scalar(sp_t, sp_t, -float(BLOCKS), None, ALU.mult))
            plink(gp.tensor_tensor(node_b, sp_r, sp_t, ALU.add))

            def clear_sums():
                nc.gpsimd.memset(aggT[0:D, 0:N + WINDOW], 0.0).then_inc(s_added, 1)

            clear_sums()
            for L in range(3):
                if L == 1:
                    pool.wait_ge(s_px, 2 + NC)
                    clear_sums()
                if L == 2:
                    pool.wait_ge(s_comb, NC)
                    clear_sums()
                for k in range(2):
                    pool.wait_ge(s_tdma[k], 16 * table_uses(k, L + 1))

                def gather(at, L=L):
                    g = at(0)
                    pool.wait_ge(s_idx, L * G + g.n + 1)
                    if L == 0:
                        pool.wait_ge(s_msg, g.n + 1)
                    else:
                        pool.wait_ge(s_agg, L * G + g.n + 1)
                    pool.sem_inc(s_go, 1)
                    for j in range(TILES):
                        nc.gpsimd.indirect_dma_start(
                            out=gath[g.slot][:, j * D:(j + 1) * D], out_offset=None, in_=table[L][:, :],
                            in_offset=bass.IndirectOffsetOnAxis(ap=idx[g.slot][:, j:j + 1], axis=0),
                        ).then_inc(s_gath[L][g.slot], 16)
                turns(pool, G, SLOTS, 0, 0, gather)

            pool.wait_ge(s_aggdone, 3)
            plink(nc.gpsimd.tensor_scalar(to_spare, src_f[:, :], 0.0, spare1[:, 0:1], ALU.is_lt, ALU.mult))
            plink(nc.gpsimd.tensor_tensor(src_f[:, :], src_f[:, :], to_spare, ALU.add))
            nc.gpsimd.tensor_scalar(to_spare, src_f[:, :], -1.0, spare[:, 0:1], ALU.mult, ALU.add).then_inc(s_lists3, 1)

            for k in range(2):
                pool.wait_ge(s_tdma[k], 16 * table_uses(k, 4))
            pool.wait_ge(s_zeroed, 16 * TILES * ((N + SPARE) // (4 * P_NODE)))

            def scatter(g):
                pool.wait_ge(s_to, g.n + 1)
                pool.wait_ge(s_totc, SLOTS + g.n + 1)
                for j in range(TILES):
                    wait_for(pool, s_scat[j], 16 * g.n)
                    pool.sem_inc(s_go, 1)
                    nc.gpsimd.indirect_dma_start(
                        out=acc[j][:, :],
                        out_offset=bass.IndirectOffsetOnAxis(ap=to_idx[g.slot][:, j:j + 1], axis=0),
                        in_=total[g.slot][:, j * D:(j + 1) * D], in_offset=None, compute_op=ALU.add,
                    ).then_inc(s_scat[j], 16)

            def gather_scatter(at):
                g, ahead = at(0), at(1)
                if ahead:
                    pool.wait_ge(s_idx, 3 * G + ahead.n + 1)
                    pool.wait_ge(s_tot, ahead.n + 1)
                    pool.sem_inc(s_go, 1)
                    for j in range(TILES):
                        nc.gpsimd.indirect_dma_start(
                            out=gath[ahead.slot][:, j * D:(j + 1) * D], out_offset=None, in_=table[3][:, :],
                            in_offset=bass.IndirectOffsetOnAxis(ap=idx[ahead.slot][:, j:j + 1], axis=0),
                        ).then_inc(s_gath[3][ahead.slot], 16)
                if g:
                    scatter(g)

            pool.wait_ge(s_spill, 1)
            with pool.If(pool.value_load(spill_i[0:1, 0:1], min_val=0, max_val=1) > 0):
                turns(pool, G, SLOTS, 1, 0, gather_scatter, peel=1)
            with pool.Else():
                turns(pool, G, SLOTS, 0, 0, lambda at: scatter(at(0)), peel=1)

        @block.scalar
        def _(act):
            def load(to, name_or_ap):
                ap = io[name_or_ap] if isinstance(name_or_ap, str) else name_or_ap
                act.dma_start(to, ap).then_inc(s_w, 16)

            def as_col(name):
                return io[name].rearrange("(p o) -> p o", o=1)

            def as_row(name):
                return io[name].rearrange("(o d) -> o d", o=1)

            act.preload_act_table_set("natural_log_exp_and_others")
            act.wait_ge(s_zero, 1)
            for o in (0, D):
                load(We1[o:o + D, o:o + D], "L0_gnn_We1")
                load(We2[o:o + D, o:o + D], "L0_gnn_We2")
                load(be1[o:o + D, 0:1], as_col("L0_gnn_be1"))
            for r in range(4):
                load(be2x[0:1, r * D:(r + 1) * D], as_row("L0_gnn_be2"))
            load(Wn[0:D, :], "L0_gnn_Wn")
            load(Wn[D:D + 1, :], as_row("L0_gnn_bn"))
            load(Wc[:, 0:D], "L0_gnn_Wc")
            load(bc[:, 0:1], as_col("L0_gnn_bc"))
            load(Wo[0:D, :], "L0_gnn_Wo")
            load(Wo[D:D + 1, :], as_row("L0_gnn_bo"))
            load(gin_W1[:, :], "L1_gnn_W1")
            load(gin_W2[:, :], "L1_gnn_W2")
            for i, v in enumerate(("b", "g", "be")):
                load(gin_v1[:, i:i + 1], as_col(f"L1_gnn_{v}1"))
                load(gin_v2[:, i:i + 1], as_col(f"L1_gnn_{v}2"))
            load(gin_eps[:, :], io["L1_gnn_epsilon"].to_broadcast([D, 1]))
            load(bi_W[0:D, :], "L2_gnn_W1")
            load(bi_W[D:2 * D, :], "L2_gnn_W2")
            load(Wp[0:D, :], "L3_gnn_W_prep")
            load(Wp[D:D + 1, :], as_row("L3_gnn_b_prep"))
            load(Wu[:, :], "L3_gnn_W_upd")
            for r in range(4):
                load(bu[0:1, r, :], as_row("L3_gnn_b_upd"))
            for i, v in enumerate(("gamma_p", "beta_p", "mean_p", "var_p", "gamma_u", "beta_u", "mean_u", "var_u")):
                load(rows3[0:1, i, :], as_row(f"L3_gnn_{v}"))
            guesses = [0]

            def rsqrt_guess(rows, cols):
                guesses[0] += 1
                n = guesses[0]
                act.wait_ge(s_rqv, n)
                act.activation(rq_l[0:rows, 0:cols], rq_v[0:rows, 0:cols], ACT.Ln).then_inc(s_rqy, 1)
                act.wait_ge(s_rqy, 2 * n - 1)
                act.activation(rq_y[0:rows, 0:cols], rq_l[0:rows, 0:cols], ACT.Exp, scale=-0.5).then_inc(s_rqy, 1)

            lists = (src_f, dst_f, w_edge)
            for i in range(3 * GR):
                a, q = i // GR, i % GR
                r = min(P, G - q * P)
                act.wait_ge(s_rowT, i + 1)
                act.activation(by_tile(lists[a][:, :]).rearrange("p g j -> p j g")[:, :, q * P:q * P + r],
                               ps[i % 2][:, :].rearrange("p (j g) -> p j g", j=TILES)[:, :, 0:r], ACT.Copy)\
                   .then_inc(s_list, 1)
            rsqrt_guess(1, D)
            rsqrt_guess(1, D)

            def make_table(L):
                rsqrt_guess(P_NODE, BLOCKS)

                def body(at):
                    c, e = at(2), at(0)
                    if c:
                        n = L * NC + c.n
                        act.wait_ge(s_hn, n + 1)
                        if L == 1:
                            wait_for(act, s_tdma[c.slot], 16 * table_uses(c.slot, L, c.round))
                            act.activation(tab[c.slot][:, :], hn[c.slot][:, :], ACT.Relu).then_inc(s_tab, 1)
                        act.wait_ge(s_tT, n + 1)
                        if L == 2:
                            act.wait_ge(s_tab, n + 1)
                        act.activation(hs[c.slot][:, :], hn[c.slot][:, :], ACT.Relu).then_inc(s_hs, 1)
                    if e:
                        n = L * NC + e.n
                        if L:
                            act.wait_ge(s_tT, n + 3)
                            if L == 3:
                                act.wait_ge(s_col, NC + e.n + 3)
                            act.activation(hT_chunk(e.n), ps[e.slot][0:D, 0:CN], ACT.Copy).then_inc(s_hT, 1)
                        if L in (0, 3):
                            act.wait_ge(s_proj, (L // 3) * NC + e.n + 3)
                            wait_for(act, s_tdma[e.slot], 16 * table_uses(e.slot, L, e.round))
                            act.activation(tab[e.slot][:, :], ps[2 + e.slot][0:P_NODE, 0:CF],
                                           ACT.Relu if L else ACT.Copy).then_inc(s_tab, 1)
                turns(act, NC, 2, 2, 0, body, peel=1)

            def stage_indices(g, of=src_f):
                act.activation(idx[g.slot][:, :], of[:, bass.ds(g.n * TILES, TILES)], ACT.Relu).then_inc(s_idx, 1)

            def stage_first(L):
                for s in range(SLOTS):
                    if L:
                        gathered(act, L - 1, Item(0, G - 1 - (G - 1 - s) % SLOTS, SLOTS))
                    stage_indices(Item(0, s, SLOTS), dst_f if L == 3 else src_f)

            make_table(0)
            stage_first(0)

            def filter_steps(at):
                g0, g1, g3, g4 = (at(o) for o in (0, 1, 3, 4))
                if g4:
                    act.wait_ge(s_eT, SLOTS + g4.n + 1)
                    act.activation(eaT[g4.slot], ps_eT, ACT.Copy).then_inc(s_eTc, 1)
                if g0 and g3:
                    gathered(act, 0, g0)
                    stage_indices(g3)
                if g1:
                    act.wait_ge(s_zb, g1.n + 1)
                    act.activation(u2[g1.slot], filt[g1.slot], ACT.Abs).then_inc(s_m2, 1)
                    act.wait_ge(s_m2, g1.n + 1)
                    act.activation(u2[g1.slot], u2[g1.slot], ACT.Exp, scale=-1.0).then_inc(s_e2, 1)
                    act.wait_ge(s_e2, g1.n + 1)
                    act.activation(u2[g1.slot], u2[g1.slot], ACT.Ln, bias=half[:, :], scale=0.5).then_inc(s_l2, 1)
                if g3:
                    act.wait_ge(s_m1, g3.n + 1)
                    act.activation(u1[g3.slot], u1[g3.slot], ACT.Exp).then_inc(s_e1, 1)
                    act.wait_ge(s_e1, g3.n + 1)
                    act.activation(u1[g3.slot], u1[g3.slot], ACT.Ln, bias=half[:, :], scale=0.5).then_inc(s_l1, 1)
            turns(act, G, SLOTS, 4, 0, filter_steps)

            def post0(at):
                c = at(0)
                act.wait_ge(s_pm, c.n + 1)
                act.activation(gcol[c.slot][0:D, :], gcol[c.slot][0:D, :], ACT.Exp).then_inc(s_pe, 1)
                act.wait_ge(s_pe, c.n + 1)
                act.activation(gcol[c.slot][0:D, :], gcol[c.slot][0:D, :], ACT.Ln, bias=half[0:D, :], scale=0.5)\
                   .then_inc(s_pl, 1)
            turns(act, NC, 2, 0, 0, post0)
            make_table(1)

            def plain_steps(L):
                stage_first(L)

                def body(at):
                    g0, g3 = at(0), at(3)
                    if g0 and g3:
                        gathered(act, L, g0)
                        stage_indices(g3)
                turns(act, G, SLOTS, 3, 0, body)

            plain_steps(1)
            rsqrt_guess(P_NODE, BLOCKS)

            def keep_hidden(at):
                c = at(0)
                act.wait_ge(s_bn, c.n + 1)
                act.activation(hidden_chunk(0, c.n), ps[c.slot][0:D, 0:CN], ACT.Copy)
                act.activation(hidden_chunk(1, c.n), ps[c.slot][D:2 * D, 0:CN], ACT.Copy).then_inc(s_hk, 1)
            turns(act, NC, 2, 0, 0, keep_hidden)
            rsqrt_guess(P, 1)
            act.wait_ge(s_bnc, 1)
            act.wait_ge(s_hk, 2 + NC)

            def hidden(at):
                c = at(0)
                act.wait_ge(s_h2, c.n + 1)
                act.activation(gcol[c.slot][0:D, :], hidden_chunk(0, c.n), ACT.Relu, bias=bn_up[D:2 * D, 1:2],
                               scale=bn_up[D:2 * D, 0:1])
                act.activation(gcol[c.slot][D:2 * D, :], hidden_chunk(1, c.n), ACT.Relu, bias=bn_sh[D:2 * D, :],
                               scale=bn_sc[D:2 * D, :]).then_inc(s_act1, 1)
            turns(act, NC, 2, 0, 0, hidden)
            rsqrt_guess(D, 1)
            act.wait_ge(s_bnc, 2)

            def gin_output(at):
                c = at(0)
                act.wait_ge(s_yT, c.n + 1)
                act.activation(col[c.slot][0:D, :], hT_chunk(c.n), ACT.Identity, bias=bn_sh[0:D, :],
                               scale=bn_sc[0:D, :]).then_inc(s_y, 1)
            turns(act, NC, 2, 0, 0, gin_output)
            make_table(2)
            plain_steps(2)

            act.wait_ge(s_aggdone, 3)

            def stage_operands(at):
                c = at(0)
                act.wait_ge(s_pb, NC + c.n + 1)
                act.activation(col[c.slot][0:D, :], hT_chunk(c.n), ACT.Copy)
                act.activation(by_block(gcol[c.slot][0:D, :]), agg_chunk(c.n), ACT.Copy).then_inc(s_stg, 1)
            turns(act, NC, 2, 0, 0, stage_operands)
            make_table(3)

            def copy_totals(g):
                act.wait_ge(s_tot, SLOTS + g.n + 1)
                scattered(act, g.n - 2)
                act.activation(total[g.slot], ps_total, ACT.Copy).then_inc(s_totc, 1)

            def window_totals(at):
                g, n = at(0), at(1)
                if n:
                    act.wait_ge(s_from, n.n + 1)
                    act.wait_ge(s_tot, n.n + 1)
                    act.activation(from_win[n.slot], ps_from[n.slot][:, :], ACT.Copy).then_inc(s_fromc, 1)
                if g:
                    copy_totals(g)

            def gathered_totals(at):
                g, ahead = at(0), at(3)
                if g:
                    copy_totals(g)
                    if ahead:
                        gathered(act, 3, g)
                        stage_indices(ahead, dst_f)

            act.wait_ge(s_spill, 1)
            with act.If(act.value_load(spill_i[0:1, 0:1], min_val=0, max_val=1) > 0):
                stage_first(3)
                turns(act, G, SLOTS, 3, 0, gathered_totals, peel=1)
            with act.Else():
                turns(act, G, SLOTS, 1, 0, window_totals, peel=1)

            def stage_update(at):
                c = at(0)
                act.wait_ge(s_pb, 2 * NC + c.n + 1)
                act.activation(gcol[c.slot][0:D, :], hT_chunk(c.n), ACT.Copy)
                act.wait_ge(s_pT, c.n + 1)
                act.activation(gcol[c.slot][D:2 * D, :], ps[4 + c.slot][0:D, 0:CN], ACT.Copy).then_inc(s_pTc, 1)
            turns(act, NC, 2, 0, 0, stage_update)

        @block.vector
        def _(dve):
            V = nc.vector
            step = [0]

            def link(ins):
                step[0] += 1
                ins.then_inc(s_setup, 1)
                dve.wait_ge(s_setup, step[0])

            for w in (We1, We2, zeros):
                V.memset(w[:, :], 0.0)
            V.memset(Wc[:, :], 0.0).then_inc(s_zero, 1)
            V.memset(last_row[:, 0:D], 0.0)
            V.memset(last_row[:, D:D + 1], 1.0)
            V.memset(ones_row[:, :], 1.0)
            V.memset(zero_row[:, :], 0.0)
            V.memset(half[:, :], 0.5)
            for k in range(2):
                V.memset(col[k][D:D + 1, :], 1.0)
            V.memset(spill[:, :], 0.0).then_inc(s_const, 1)
            for s in (s_hs, s_tT, s_hT, s_col, s_proj, s_tab, s_sp, s_pb, s_px, s_hk, s_act1, s_h2, s_h2k, s_yT,
                      s_t2, s_pavg):
                dve.sem_inc(s, 2)
            for s in (s_eT, s_msg, s_agg, s_added, s_cnt, s_same, s_tot, s_totc):
                dve.sem_inc(s, SLOTS)
            dve.wait_ge(s_ident, 4)
            dve.wait_ge(s_iota, 2)
            link(V.tensor_copy(iota_f[:, :], iota_i))
            link(V.tensor_copy(spare[:, :], spare_i[:, :]))
            link(V.tensor_scalar(spare1[:, :], spare[:, :], 1.0, None, ALU.add))

            def layer_stats(L, c):
                if c:
                    dve.wait_ge(s_px, 2 + (L - 1) * NC + c.n + 1 if L else 2)
                    for j in range(CB):
                        b = c.n * CB + j
                        ins = V.bn_stats(stats[:, bass.ds(b, 1), :].rearrange("p o s -> p (o s)"),
                                         x_nm[:, bass.ds(b * D, D)])
                    ins.then_inc(s_stat, 1)

            dve.wait_ge(s_x, 32)
            turns(dve, NC, 2, 0, 0, lambda at: layer_stats(0, at(0)))

            rq = [0, 0]

            def rsqrt(rows, cols, out):
                rq[0] += 1
                dve.wait_ge(s_rqy, 2 * rq[0])
                v, y, t = (z[0:rows, 0:cols] for z in (rq_v, rq_y, rq_t))

                def newton(ins):
                    rq[1] += 1
                    ins.then_inc(s_rqn, 1)
                    dve.wait_ge(s_rqn, rq[1])
                newton(V.tensor_tensor(t, y, y, ALU.mult))
                newton(V.tensor_tensor(t, t, v, ALU.mult))
                newton(V.tensor_scalar(t, t, -0.5, 1.5, ALU.mult, ALU.add))
                newton(V.tensor_tensor(out, y, t, ALU.mult))

            dve.wait_ge(s_w, 16 * 42)
            link(V.tensor_scalar(be1[:, 1:2], be1[:, 0:1], -LOG2, None, ALU.add))
            link(V.tensor_scalar(bc[:, 1:2], bc[:, 0:1], -LOG2, None, ALU.add))
            for i in range(2):
                gamma, beta, mu, var = (rows3[0:1, 4 * i + j, :] for j in range(4))
                scale, shift, t = fold[0:1, 2 * i, :], fold[0:1, 2 * i + 1, :], rq_t[0:1, 0:D]
                V.tensor_scalar(rq_v[0:1, 0:D], var, BN3_EPS, None, ALU.add).then_inc(s_rqv, 1)
                rsqrt(1, D, scale)
                link(V.tensor_tensor(scale, scale, gamma, ALU.mult))
                link(V.tensor_tensor(t, mu, scale, ALU.mult))
                link(V.tensor_tensor(shift, beta, t, ALU.subtract))
            for r in range(4):
                link(V.tensor_tensor(bu[0:1, r, :], bu[0:1, r, :], fold[0:1, 2, :], ALU.mult))
                link(V.tensor_tensor(bu[0:1, r, :], bu[0:1, r, :], fold[0:1, 3, :], ALU.add))
            dve.sem_inc(s_fold, 1)
            dve.wait_ge(s_foldb, 1)
            V.tensor_copy(be2b[:, :], ps[6][:, 0:4 * D])
            V.tensor_copy(bu_b[:, :], ps[6][:, 4 * D:8 * D])
            link(V.tensor_tensor(Wp[:, :], Wp[:, :], ps[4][0:D + 1, 0:D], ALU.mult))
            link(V.tensor_tensor(Wp[:, :], Wp[:, :], ps[5][0:D + 1, 0:D], ALU.add))
            link(V.tensor_tensor(Wu[:, :], Wu[:, :], ps[4][:, P:P + D], ALU.mult))
            dve.wait_ge(s_list, 3 * GR)
            V.tensor_scalar(base_f, by_tile(dst_f[:, :])[0:1, :, 0], float(N - WINDOW), None, ALU.min)\
             .then_inc(s_dstf, 1)
            dve.wait_ge(s_dstf, 1)
            link(V.tensor_copy(base_i[0:1, :], base_f))
            dve.wait_ge(s_baseb, 1)
            link(V.tensor_tensor(by_tile(dst_rel[:, :]), by_tile(dst_f[:, :]), spread(ps[2][:, 0:G], TILES),
                                 ALU.subtract))
            link(V.tensor_scalar(sp_t, dst_rel[:, :], float(WINDOW), None, ALU.is_ge))
            link(V.tensor_reduce(spill[:, 0:1], sp_t, AX.X, ALU.max))
            link(V.tensor_scalar(sp_t, dst_rel[:, :], 0.0, None, ALU.is_lt))
            link(V.scalar_tensor_tensor(sp_t, dst_f[:, :], 0.0, sp_t, ALU.is_ge, ALU.mult))
            link(V.tensor_reduce(spill[:, 1:2], sp_t, AX.X, ALU.max))
            V.tensor_tensor(spill[:, 2:3], spill[:, 0:1], spill[:, 1:2], ALU.max).then_inc(s_flags, 1)
            dve.wait_ge(s_flagT, 1)
            link(V.tensor_reduce(spill[0:1, 4:5], ps[3][0:1, 0:P], AX.X, ALU.max))
            V.tensor_copy(spill_i[:, :], spill[0:1, 4:5]).then_inc(s_spill, 1)
            dve.sem_inc(s_ready, 1)

            def make_table(L):
                dve.wait_ge(s_stat, (L + 1) * NC)
                v = rq_v[0:P_NODE, 0:BLOCKS]
                link(V.tensor_tensor(mean[:, :], stats[:, :, 1], stats[:, :, 4], ALU.add))
                link(V.tensor_tensor(rstd[:, :], stats[:, :, 1], stats[:, :, 4], ALU.subtract))
                link(V.tensor_scalar(mean[:, :], mean[:, :], 0.5, None, ALU.mult))
                link(V.tensor_tensor(rstd[:, :], rstd[:, :], rstd[:, :], ALU.mult))
                link(V.tensor_tensor(v, stats[:, :, 2], stats[:, :, 5], ALU.add))
                link(V.tensor_scalar(v, v, 1.0 / D, LN_EPS, ALU.mult, ALU.add))
                V.scalar_tensor_tensor(v, rstd[:, :], 0.25, v, ALU.mult, ALU.add).then_inc(s_rqv, 1)
                rsqrt(P_NODE, BLOCKS, rstd[:, :])

                def body(at):
                    c, e = at(2), at(0)
                    if c:
                        dve.wait_ge(s_hs, L * NC + c.n + 1)
                        for j in range(CB):
                            b = c.n * CB + j
                            ins = V.tensor_scalar(hn[c.slot][:, j * D:(j + 1) * D], x_nm[:, bass.ds(b * D, D)],
                                                  mean[:, bass.ds(b, 1)], rstd[:, bass.ds(b, 1)],
                                                  ALU.subtract, ALU.mult)
                        ins.then_inc(s_hn, 1)
                    if e and L in (0, 3):
                        m = (L // 3) * NC + e.n
                        dve.wait_ge(s_tT, L * NC + e.n + 3)
                        dve.wait_ge(s_proj, m + 1)
                        V.tensor_copy(col[e.slot][0:D, :], ps[e.slot][0:D, 0:CN]).then_inc(s_col, 1)
                    if e and L == 2:
                        dve.wait_ge(s_hs, L * NC + e.n + 3)
                        dve.wait_ge(s_tdma[e.slot], 16 * table_uses(e.slot, L, e.round))
                        V.tensor_tensor(by_block(tab[e.slot][:, :]), by_block(hs[e.slot][:, :]),
                                        spread(rs_deg[:, bass.ds(e.n * CB, CB)], D), ALU.mult).then_inc(s_tab, 1)
                turns(dve, NC, 2, 2, 0, body)

            make_table(0)
            dve.wait_ge(s_spill, 1)
            spilled = dve.value_load(spill_i[0:1, 0:1], min_val=0, max_val=1)

            def dst_onehots(to, dst, at):
                for j in range(TILES):
                    ins = V.tensor_scalar(to[:, j * WINDOW:(j + 1) * WINDOW], iota_f[:, :], dst[:, bass.ds(at + j, 1)],
                                          None, ALU.is_equal)
                return ins

            def count_onehots(g):
                dve.wait_ge(s_cnt, g.n + 1)
                for j in range(TILES):
                    e = g.n * TILES + j
                    V.tensor_scalar(one_p[g.slot][:, j, :], iota_f[:, :], node_p[:, bass.ds(e, 1)],
                                    None, ALU.is_equal)
                    ins = V.tensor_scalar(one_b[g.slot][:, j, :], iota_f[:, 0:BLOCKS],
                                          node_b[:, bass.ds(e, 1)], None, ALU.is_equal)
                ins.then_inc(s_cntoh, 1)

            def start_filters(g1, g3):
                if g1:
                    dve.wait_ge(s_z2, g1.n + 1)
                    V.tensor_tensor(filt[g1.slot], ps_z2, be2b[:, :], ALU.add).then_inc(s_zb, 1)
                if g3:
                    dve.wait_ge(s_z1, g3.n + 1)
                    V.tensor_scalar(u1[g3.slot], ps_z1[g3.slot], be1[:, 0:1], CLAMP, ALU.add, ALU.min).then_inc(s_m1, 1)

            def finish_second(g):
                dve.wait_ge(s_l2, g.n + 1)
                V.scalar_tensor_tensor(filt[g.slot], filt[g.slot], 0.0, u2[g.slot], ALU.max, ALU.add).then_inc(s_f, 1)
                gathered(dve, 0, g)
                dve.wait_ge(s_f, g.n + 1)
                V.tensor_tensor(filt[g.slot], filt[g.slot], gath[g.slot], ALU.mult).then_inc(s_msg, 1)

            def finish_first(g2):
                if g2:
                    dve.wait_ge(s_l1, g2.n + 1)
                    V.scalar_tensor_tensor(a1[g2.slot], ps_z1[g2.slot], be1[:, 1:2], u1[g2.slot], ALU.add, ALU.max)\
                     .then_inc(s_a1, 1)

            def fast_steps(L):
                def body(at):
                    prev, g = at(-1), at(0)
                    if L == 0 and g:
                        finish_second(g)
                    if g:
                        dve.wait_ge(s_agg, L * G + g.n + 1)
                        dst_onehots(onehot[g.slot], dst_rel, g.n * TILES).then_inc(s_oh, 1)
                        if L == 1:
                            count_onehots(g)
                    if L == 0:
                        finish_first(at(2))
                        start_filters(at(1), at(3))
                    if prev:
                        first = dve.value_load(base_i[0:1, bass.ds(prev.n, 1)], min_val=0, max_val=N - WINDOW)
                        dve.wait_ge(s_agg, SLOTS + L * G + prev.n + 1)
                        dve.wait_ge(s_added, SLOTS + L * (G + 1) + prev.n + 1)
                        w = aggT[0:D, bass.ds(first, WINDOW)]
                        V.tensor_tensor(w, w, ps_agg[prev.slot], ALU.add).then_inc(s_added, 1)
                turns(dve, G, SLOTS, 3 if L == 0 else 0, 1, body)

            def general_steps(L):
                def body(at):
                    g = at(0)
                    if L == 0:
                        if g:
                            finish_second(g)
                        finish_first(at(2))
                        start_filters(at(1), at(3))
                    if not g:
                        return
                    if L == 1:
                        count_onehots(g)
                    done = (L * G + g.n) * NW
                    shifts = (L * G + g.n) * (NW + 1)
                    V.tensor_copy(wdst[:, :], dst_f[:, bass.ds(g.n * TILES, TILES)]).then_inc(s_gdst, 1)
                    with dve.Fori(0, NW) as w:
                        dve.wait_ge(s_gdst, shifts + w + 1)
                        dst_onehots(onehot[0], wdst, 0).then_inc(s_goh, 1)
                        dve.wait_ge(s_gsum, done + w + 1)
                        win = aggT[0:D, bass.ds(w * WINDOW, WINDOW)]
                        V.tensor_tensor(win, win, ps_agg[0], ALU.add).then_inc(s_gadd, 1)
                        V.tensor_scalar(wdst[:, :], wdst[:, :], -float(WINDOW), None, ALU.add).then_inc(s_gdst, 1)
                    dve.wait_ge(s_gadd, done + NW)
                    dve.wait_ge(s_gdst, shifts + NW + 1)
                turns(dve, G, SLOTS, 3 if L == 0 else 0, 0, body)
                dve.sem_inc(s_added, G)

            def aggregate(L):
                dve.wait_ge(s_added, SLOTS + L * (G + 1) + 1)
                with dve.If(spilled > 0):
                    general_steps(L)
                with dve.Else():
                    fast_steps(L)
                dve.wait_ge(s_added, SLOTS + (L + 1) * (G + 1))
                dve.sem_inc(s_aggdone, 1)

            aggregate(0)

            def post0(at):
                p, c, n = at(-1), at(0), at(1)
                if c:
                    dve.wait_ge(s_pl, c.n + 1)
                    dve.wait_ge(s_pb, c.n + 1)
                    V.scalar_tensor_tensor(col[c.slot][0:D, :], ps[c.slot][0:D, 0:CN], bc[:, 1:2],
                                           gcol[c.slot][0:D, :], ALU.add, ALU.max).then_inc(s_sp, 1)
                if p:
                    dve.wait_ge(s_pb, p.n + 3)
                    V.tensor_tensor(x_chunk(p.n), x_chunk(p.n), ps[2 + p.slot][0:P_NODE, 0:CF], ALU.add)\
                     .then_inc(s_px, 1)
                if n:
                    dve.wait_ge(s_pa, n.n + 1)
                    V.tensor_scalar(gcol[n.slot][0:D, :], ps[n.slot][0:D, 0:CN], bc[:, 0:1], CLAMP, ALU.add, ALU.min)\
                     .then_inc(s_pm, 1)
                layer_stats(1, at(-2))
            turns(dve, NC, 2, 1, 2, post0)
            make_table(1)
            aggregate(1)
            dve.wait_ge(s_cntall, 1)
            V.tensor_scalar(rq_v[0:P_NODE, 0:BLOCKS], ps_count, 1.0, None, ALU.max).then_inc(s_rqv, 1)
            rsqrt(P_NODE, BLOCKS, rs_deg[:, :])
            link(V.tensor_scalar(rc_deg[:, :], ps_count, 1.0, None, ALU.max))
            link(V.reciprocal(rc_deg[:, :], rc_deg[:, :]))

            link(V.tensor_scalar(gin_eps[:, :], gin_eps[:, :], 1.0, None, ALU.add))
            dve.wait_ge(s_hT, 2 + NC)

            def combine(at):
                c, n = at(0), at(1)
                if n:
                    h = by_block(hT_chunk(n.n))
                    V.scalar_tensor_tensor(h, h, gin_eps[:, 0:1], agg_chunk(n.n), ALU.mult, ALU.add).then_inc(s_comb, 1)
                if c:
                    dve.wait_ge(s_h1, c.n + 1)
                    V.bn_stats(bn_raw[:, bass.ds(c.n, 1), :].rearrange("p o s -> p (o s)"), ps[c.slot][:, 0:CN])\
                     .then_inc(s_bn, 1)
            turns(dve, NC, 2, 1, 0, combine)
            dve.wait_ge(s_bn, NC)

            def batch_constants(rows, vec):
                t, sc = bn_t[0:rows, :], bn_sc[0:rows, :]
                link(V.bn_aggr(bn_mv[0:rows, :], bn_raw[0:rows, :, :].rearrange("p a b -> p (a b)")))
                V.tensor_scalar(rq_v[0:rows, 0:1], bn_mv[0:rows, 1:2], BN1_EPS, None, ALU.add).then_inc(s_rqv, 1)
                rsqrt(rows, 1, t)
                link(V.tensor_tensor(sc, t, vec[0:rows, 1:2], ALU.mult))
                link(V.tensor_tensor(t, bn_mv[0:rows, 0:1], vec[0:rows, 0:1], ALU.add))
                link(V.tensor_tensor(t, vec[0:rows, 0:1], t, ALU.subtract))
                link(V.tensor_tensor(t, t, sc, ALU.mult))
                link(V.tensor_tensor(bn_sh[0:rows, :], t, vec[0:rows, 2:3], ALU.add))
                V.tensor_copy(bn_up[D:2 * D, 0:1], bn_sc[0:D, :])
                V.tensor_copy(bn_up[D:2 * D, 1:2], bn_sh[0:D, :]).then_inc(s_bnc, 1)
            batch_constants(P, gin_v1)

            def keep_second(at):
                c = at(0)
                dve.wait_ge(s_h2, c.n + 3)
                V.tensor_copy(hT_chunk(c.n), ps[2 + c.slot][0:D, 0:CN])
                V.bn_stats(bn_raw[0:D, bass.ds(c.n, 1), :].rearrange("p o s -> p (o s)"), ps[2 + c.slot][0:D, 0:CN])\
                 .then_inc(s_h2k, 1)
            turns(dve, NC, 2, 0, 0, keep_second)
            dve.wait_ge(s_h2k, 2 + NC)
            batch_constants(D, gin_v2)

            def post1(at):
                c = at(0)
                if c:
                    dve.wait_ge(s_yT, c.n + 3)
                    V.tensor_tensor(x_chunk(c.n), x_chunk(c.n), ps[4 + c.slot][0:P_NODE, 0:CF], ALU.add)\
                     .then_inc(s_px, 1)
                layer_stats(2, at(-1))
            turns(dve, NC, 2, 0, 1, post1)
            make_table(2)
            aggregate(2)
            dve.wait_ge(s_hT, 2 + 2 * NC)

            def post2(at):
                c, n = at(0), at(2)
                if n:
                    dve.wait_ge(s_pb, NC + n.n + 1)
                    V.tensor_tensor(by_block(gcol[n.slot][D:2 * D, :]), by_block(hT_chunk(n.n)), agg_chunk(n.n),
                                    ALU.mult).then_inc(s_hg, 1)
                if c:
                    own, nbr = ps[c.slot][0:P_NODE, 0:CF], ps[2 + c.slot][0:P_NODE, 0:CF]
                    t = hn[c.slot][:, :]
                    dve.wait_ge(s_pb, NC + c.n + 3)
                    V.tensor_tensor(by_block(t), by_block(nbr), spread(rs_deg[:, bass.ds(c.n * CB, CB)], D), ALU.mult)\
                     .then_inc(s_t1, 1)
                    dve.wait_ge(s_t1, c.n + 1)
                    V.tensor_tensor(t, t, own, ALU.add).then_inc(s_t2, 1)
                    dve.wait_ge(s_t2, c.n + 3)
                    V.scalar_tensor_tensor(t, t, LEAKY, t, ALU.mult, ALU.max).then_inc(s_t3, 1)
                    dve.wait_ge(s_t3, c.n + 1)
                    V.tensor_tensor(x_chunk(c.n), x_chunk(c.n), t, ALU.add).then_inc(s_px, 1)
                layer_stats(3, at(-1))
            turns(dve, NC, 2, 2, 1, post2)
            make_table(3)

            def total_steps(window):
                def body(at):
                    n, ahead = at(1), at(2)
                    if ahead:
                        wait_for(dve, s_bsrc, ahead.n - 2)
                        V.tensor_copy(srcs[ahead.slot], src_f[:, bass.ds(ahead.n * TILES, TILES)]).then_inc(s_srcs, 1)
                    if not n:
                        return
                    dve.wait_ge(s_tot, n.n + 1)
                    if window:
                        for j in range(TILES):
                            e = n.n * TILES + j
                            ins = V.tensor_scalar(onehot[n.slot][:, j * P:(j + 1) * P], iota_f[:, :],
                                                  dst_rel[:, bass.ds(e, 1)], w_edge[:, bass.ds(e, 1)],
                                                  ALU.is_equal, ALU.mult)
                        ins.then_inc(s_ohw, 1)
                    dve.wait_ge(s_bsrc, n.n + 1)
                    for j in range(TILES):
                        tile = slice(j * P, (j + 1) * P)
                        ins = V.scalar_tensor_tensor(same[n.slot][:, tile], ps_src[n.slot][:, tile],
                                                     srcs[n.slot][:, j:j + 1], upper[:, :],
                                                     ALU.is_equal, ALU.mult, accum_out=later[n.slot][:, j:j + 1])
                    ins.then_inc(s_same, 1)
                    dve.wait_ge(s_same, SLOTS + n.n + 1)
                    V.scalar_tensor_tensor(later[n.slot][:, :], later[n.slot][:, :], 1.5,
                                           to_spare[:, bass.ds(n.n * TILES, TILES)], ALU.is_gt, ALU.mult)\
                     .then_inc(s_dup, 1)
                    if not window:
                        gathered(dve, 3, n)
                        rows = gath[n.slot].rearrange("p (j d) -> p j d", j=TILES)
                        V.tensor_tensor(rows, rows, spread(w_edge[:, bass.ds(n.n * TILES, TILES)], D), ALU.mult)\
                         .then_inc(s_wrow, 1)
                    dve.wait_ge(s_dup, n.n + 1)
                    scattered(dve, n.n - 2)
                    V.tensor_tensor(to_idx[n.slot][:, :], later[n.slot][:, :], srcs[n.slot], ALU.add).then_inc(s_to, 1)
                turns(dve, G, SLOTS, 2, 0, body, peel=1)

            dve.wait_ge(s_lists3, 1)
            with dve.If(spilled > 0):
                total_steps(window=False)
            with dve.Else():
                total_steps(window=True)
            scattered(dve, G)
            dve.sem_inc(s_aggdone, 1)

            def post3(at):
                c, n = at(0), at(1)
                if n:
                    parts = part[n.slot]
                    dve.wait_ge(s_part[n.slot], 16 * TILES * (n.round + 1))
                    V.tensor_tensor(parts[0], parts[0], parts[1], ALU.add).then_inc(s_psum, 1)
                    V.tensor_tensor(parts[2], parts[2], parts[3], ALU.add).then_inc(s_psum, 1)
                    dve.wait_ge(s_psum, 3 * n.n + 2)
                    V.tensor_tensor(parts[0], parts[0], parts[2], ALU.add).then_inc(s_psum, 1)
                    dve.wait_ge(s_psum, 3 * n.n + 3)
                    wait_for(dve, s_pT, n.n - 1)
                    V.tensor_tensor(by_block(hn[n.slot][:, :]), by_block(parts[0]),
                                    spread(rc_deg[:, bass.ds(n.n * CB, CB)], D), ALU.mult).then_inc(s_pavg, 1)
                if c:
                    dve.wait_ge(s_pb, 2 * NC + c.n + 3)
                    V.tensor_tensor(tab[c.slot][:, :], ps[c.slot][0:P_NODE, 0:CF], bu_b[0:P_NODE, :], ALU.add)\
                     .then_inc(s_ub, 1)
                    dve.wait_ge(s_ub, c.n + 1)
                    V.scalar_tensor_tensor(x_chunk(c.n), tab[c.slot][:, :], 0.0, x_chunk(c.n),
                                           ALU.max, ALU.add).then_inc(s_px, 1)
            turns(dve, NC, 2, 1, 0, post3, peel=1)

        @block.tensor
        def _(pe):
            T = nc.tensor
            pe.wait_ge(s_ident, 2)
            for i in range(3 * GR):
                a, q = i // GR, i % GR
                r = min(P, G - q * P)
                if a < 2:
                    pe.wait_ge(s_rowf, i + 1)
                if i >= 2:
                    pe.wait_ge(s_list, i - 1)
                rows = row_float(a, q)[0:r, :].rearrange("g (e j) -> g j e", j=TILES)
                for j in range(TILES):
                    ins = T.transpose(ps[i % 2][:, j * P:j * P + r], rows[:, j, :], ident[0:r, 0:r])
                ins.then_inc(s_rowT, 1)
            pe.wait_ge(s_const, 1)
            pe.wait_ge(s_fold, 1)
            for o, row in ((0, be2x[0:1, :]), (4 * D, bu[:, :, :].rearrange("p r d -> p (r d)"))):
                T.matmul(ps[6][:, o:o + 4 * D], ones_row[0:1, :], row, start=True, stop=True)
            T.matmul(ps[4][:, P:P + D], ones_row[0:1, :], fold[0:1, 2, :], start=True, stop=True)
            T.matmul(ps[4][0:D + 1, 0:D], ones_row[0:1, 0:D + 1], fold[0:1, 0, :], start=True, stop=True)
            ins = T.matmul(ps[5][0:D + 1, 0:D], last_row[0:1, :], fold[0:1, 1, :], start=True, stop=True)
            ins.then_inc(s_foldb, 1)
            pe.wait_ge(s_dstf, 1)
            T.matmul(ps[2][:, 0:G], ones_row[0:1, :], base_f, start=True, stop=True)\
             .then_inc(s_baseb, 1)
            pe.wait_ge(s_flags, 1)
            T.transpose(ps[3][0:1, 0:P], spill[:, 2:3], ident[:, :]).then_inc(s_flagT, 1)
            pe.wait_ge(s_ready, 1)

            def make_table(L):
                def body(at):
                    c, ahead = at(0), at(1)
                    if ahead:
                        n = L * NC + ahead.n
                        pe.wait_ge(s_hs, n + 3)
                        if L:
                            pe.wait_ge(s_hT, (L - 1) * NC + ahead.n + 1)
                        if L in (0, 3):
                            pe.wait_ge(s_col, (L // 3) * NC + ahead.n + 1)
                        pe.sem_inc(s_go, 1)
                        for j in range(CB):
                            ins = T.transpose(ps[ahead.slot][0:D, j * P_NODE:(j + 1) * P_NODE],
                                              hs[ahead.slot][:, j * D:(j + 1) * D], ident[0:P_NODE, 0:P_NODE])
                        ins.then_inc(s_tT, 1)
                    if c and L in (0, 3):
                        pe.wait_ge(s_col, (L // 3) * NC + c.n + 3)
                        pe.wait_ge(s_tab, L * NC + c.n + 1)
                        for j in range(CB):
                            ins = T.matmul(ps[2 + c.slot][0:P_NODE, j * D:(j + 1) * D],
                                           col[c.slot][:, j * P_NODE:(j + 1) * P_NODE], (Wp if L else Wn)[:, :],
                                           start=True, stop=True)
                        ins.then_inc(s_proj, 1)
                turns(pe, NC, 2, 1, 0, body)
                pe.wait_ge(s_tab, 2 + (L + 1) * NC)
                if L:
                    pe.wait_ge(s_hT, 2 + L * NC)

            make_table(0)
            pe.wait_ge(s_spill, 1)
            spilled = pe.value_load(spill_i[0:1, 0:1], min_val=0, max_val=1)

            def first_product(g3, g4):
                if g3:
                    pe.wait_ge(s_eTc, g3.n + 1)
                    wait_for(pe, s_a1, g3.n - 2)
                    T.matmul(ps_z1[g3.slot], We1[:, :], eaT[g3.slot], start=True, stop=True).then_inc(s_z1, 1)
                if g4:
                    pe.wait_ge(s_ea[g4.slot], 16 * (g4.round + 1))
                    wait_for(pe, s_eTc, g4.n)
                    for h in range(2):
                        ins = T.transpose(ps_eT[:, h * P:(h + 1) * P], eat[g4.slot][:, h * P:(h + 1) * P], ident[:, :])
                    ins.then_inc(s_eT, 1)

            def second_product(g2):
                if g2:
                    pe.wait_ge(s_a1, g2.n + 1)
                    wait_for(pe, s_zb, g2.n)
                    for h in range(2):
                        ins = T.matmul(ps_z2[:, h * P:(h + 1) * P], a1[g2.slot][:, h * P:(h + 1) * P], We2[:, :],
                                       start=True, stop=True)
                    ins.then_inc(s_z2, 1)

            def rows_ready(L, g):
                if L == 0:
                    pe.wait_ge(s_msg, SLOTS + g.n + 1)
                else:
                    gathered(pe, L, g)

            def sum_window(L, g, slot):
                rows = filt[g.slot] if L == 0 else gath[g.slot]
                for j in range(TILES):
                    ins = T.matmul(ps_agg[slot], rows[:, j * D:(j + 1) * D],
                                   onehot[slot][:, j * WINDOW:(j + 1) * WINDOW],
                                   start=(j == 0), stop=(j == TILES - 1))
                return ins

            def count_step(g):
                pe.wait_ge(s_cntoh, g.n + 1)
                for j in range(TILES):
                    ins = T.matmul(ps_count, one_p[g.slot][:, j, 0:P_NODE], one_b[g.slot][:, j, :],
                                   start=False, stop=False, skip_group_check=True)
                ins.then_inc(s_cnt, 1)

            def fast_steps(L):
                def body(at):
                    g = at(0)
                    if L == 0:
                        first_product(at(3), at(4))
                    if g:
                        step(g)
                    if L == 0:
                        second_product(at(2))

                def step(g):
                    if L == 1:
                        count_step(g)
                    rows_ready(L, g)
                    pe.wait_ge(s_oh, L * G + g.n + 1)
                    pe.wait_ge(s_added, L * (G + 1) + g.n + 2)
                    sum_window(L, g, g.slot).then_inc(s_agg, 1)
                turns(pe, G, SLOTS, 4 if L == 0 else 0, 0, body, peel=1)

            def general_steps(L):
                def body(at):
                    g = at(0)
                    if L == 0:
                        first_product(at(3), at(4))
                    if g:
                        step(g)
                    if L == 0:
                        second_product(at(2))

                def step(g):
                    if L == 1:
                        count_step(g)
                    rows_ready(L, g)
                    done = (L * G + g.n) * NW
                    pe.sem_inc(s_go, 1)
                    with pe.Fori(0, NW) as w:
                        pe.wait_ge(s_goh, done + w + 1)
                        sum_window(L, g, 0).then_inc(s_gsum, 1)
                    pe.drain().then_inc(s_agg, 1)
                turns(pe, G, SLOTS, 4 if L == 0 else 0, 0, body, peel=1)

            def aggregate(L):
                if L == 1:
                    T.matmul(ps_count, zero_row[0:1, 0:P_NODE], zero_row[0:1, 0:BLOCKS], start=True, stop=False,
                             skip_group_check=True)
                with pe.If(spilled > 0):
                    general_steps(L)
                with pe.Else():
                    fast_steps(L)
                if L == 1:
                    T.matmul(ps_count, zero_row[0:1, 0:P_NODE], zero_row[0:1, 0:BLOCKS], start=False, stop=True,
                             skip_group_check=True).then_inc(s_cntall, 1)
                pe.wait_ge(s_aggdone, L + 1)

            aggregate(0)

            def post0(at):
                c, n = at(0), at(1)
                if n:
                    pe.wait_ge(s_sp, n.n + 1)
                    T.matmul(ps[n.slot][:, 0:CN], Wc[:, :], agg_chunk(n.n), start=True, stop=True).then_inc(s_pa, 1)
                if c:
                    pe.wait_ge(s_sp, c.n + 3)
                    pe.wait_ge(s_px, c.n + 1)
                    for j in range(CB):
                        ins = T.matmul(ps[2 + c.slot][0:P_NODE, j * D:(j + 1) * D],
                                       col[c.slot][:, j * P_NODE:(j + 1) * P_NODE], Wo[:, :], start=True, stop=True)
                    ins.then_inc(s_pb, 1)
            turns(pe, NC, 2, 1, 0, post0)
            make_table(1)
            aggregate(1)

            def hidden(at):
                c = at(0)
                pe.wait_ge(s_comb, c.n + 1)
                pe.wait_ge(s_hk, c.n + 1)
                T.matmul(ps[c.slot][:, 0:CN], gin_W1[:, :], hT_chunk(c.n), start=True, stop=True).then_inc(s_h1, 1)
            turns(pe, NC, 2, 0, 0, hidden)

            def second(at):
                c = at(0)
                pe.wait_ge(s_act1, c.n + 3)
                pe.wait_ge(s_h2k, c.n + 1)
                T.matmul(ps[2 + c.slot][0:D, 0:CN], gin_W2[:, :], gcol[c.slot][:, :], start=True, stop=True)\
                 .then_inc(s_h2, 1)
            turns(pe, NC, 2, 0, 0, second)

            def gin_output(at):
                c = at(0)
                pe.wait_ge(s_y, c.n + 1)
                pe.wait_ge(s_px, NC + c.n + 1)
                pe.sem_inc(s_go, 1)
                for j in range(CB):
                    ins = T.transpose(ps[4 + c.slot][0:P_NODE, j * D:(j + 1) * D],
                                      col[c.slot][0:D, j * P_NODE:(j + 1) * P_NODE], ident[0:D, 0:D])
                ins.then_inc(s_yT, 1)
            turns(pe, NC, 2, 0, 0, gin_output)
            make_table(2)
            aggregate(2)

            def products(at):
                c = at(0)
                own, nbr = ps[c.slot], ps[2 + c.slot]
                pe.wait_ge(s_stg, c.n + 1)
                pe.wait_ge(s_hg, c.n + 1)
                pe.wait_ge(s_t2, c.n + 1)
                for j in range(CB):
                    nodes, out = slice(j * P_NODE, (j + 1) * P_NODE), slice(j * D, (j + 1) * D)
                    T.matmul(own[0:P_NODE, out], col[c.slot][0:D, nodes], bi_W[0:D, :], start=True, stop=True)
                    ins = T.matmul(nbr[0:P_NODE, out], gcol[c.slot][:, nodes], bi_W[:, :], start=True, stop=True)
                ins.then_inc(s_pb, 1)
            turns(pe, NC, 2, 0, 0, products)
            make_table(3)

            def broadcast_src(n):
                if n:
                    pe.wait_ge(s_srcs, n.n + 1)
                    pe.wait_ge(s_same, n.n + 1)
                    pe.sem_inc(s_go, 1)
                    for j in range(TILES):
                        ins = T.transpose(ps_src[n.slot][:, j * P:(j + 1) * P],
                                          srcs[n.slot][:, j:j + 1].to_broadcast([P, P]), ident[:, :])
                    ins.then_inc(s_bsrc, 1)

            def totals_from(g, matrix, rows):
                pe.wait_ge(s_totc, SLOTS + g.n)
                for j in range(TILES):
                    ins = T.matmul(ps_total[:, j * D:(j + 1) * D], matrix[g.slot][:, j * P:(j + 1) * P],
                                   rows(j), start=True, stop=True)
                ins.then_inc(s_tot, 1)

            def window_totals(at):
                g, n = at(0), at(1)
                broadcast_src(at(2))
                if g:
                    pe.wait_ge(s_win[g.slot], 16 * (g.round + 1))
                    pe.wait_ge(s_fromc, g.n + 1)
                    totals_from(g, from_win, lambda j: win[g.slot])
                if n:
                    pe.wait_ge(s_same, SLOTS + n.n + 1)
                    pe.wait_ge(s_ohw, n.n + 1)
                    wait_for(pe, s_fromc, n.n - 2)
                    for j in range(TILES):
                        tile = slice(j * P, (j + 1) * P)
                        ins = T.matmul(ps_from[n.slot][:, tile], onehot[n.slot][:, tile], same[n.slot][:, tile],
                                       start=True, stop=True)
                    ins.then_inc(s_from, 1)

            def gathered_totals(at):
                g = at(0)
                broadcast_src(at(2))
                if g:
                    pe.wait_ge(s_same, SLOTS + g.n + 1)
                    pe.wait_ge(s_wrow, g.n + 1)
                    totals_from(g, same, lambda j: gath[g.slot][:, j * D:(j + 1) * D])

            with pe.If(spilled > 0):
                turns(pe, G, SLOTS, 2, 0, gathered_totals, peel=1)
            with pe.Else():
                turns(pe, G, SLOTS, 2, 0, window_totals, peel=1)

            def update(at):
                c, n = at(0), at(1)
                if c:
                    pe.wait_ge(s_pTc, c.n + 1)
                    pe.wait_ge(s_px, 3 * NC + c.n + 1)
                    for j in range(CB):
                        nodes, out = slice(j * P_NODE, (j + 1) * P_NODE), slice(j * D, (j + 1) * D)
                        ins = T.matmul(ps[c.slot][0:P_NODE, out], gcol[c.slot][:, nodes], Wu[:, :],
                                       start=True, stop=True)
                    ins.then_inc(s_pb, 1)
                if n:
                    pe.wait_ge(s_pavg, n.n + 3)
                    wait_for(pe, s_pTc, n.n - 1)
                    pe.sem_inc(s_go, 1)
                    for j in range(CB):
                        ins = T.transpose(ps[4 + n.slot][0:D, j * P_NODE:(j + 1) * P_NODE],
                                          hn[n.slot][:, j * D:(j + 1) * D], ident[0:P_NODE, 0:P_NODE])
                    ins.then_inc(s_pT, 1)
            turns(pe, NC, 2, 1, 0, update, peel=1)


INPUTS = ["x", "src", "dst", "edge_attr_64", "edge_weight", "L0_gnn_We1", "L0_gnn_be1", "L0_gnn_We2", "L0_gnn_be2",
          "L0_gnn_Wn", "L0_gnn_bn", "L0_gnn_Wc", "L0_gnn_bc", "L0_gnn_Wo", "L0_gnn_bo", "L1_gnn_epsilon", "L1_gnn_W1",
          "L1_gnn_b1", "L1_gnn_g1", "L1_gnn_be1", "L1_gnn_W2", "L1_gnn_b2", "L1_gnn_g2", "L1_gnn_be2", "L2_gnn_W1",
          "L2_gnn_W2", "L3_gnn_W_prep", "L3_gnn_b_prep", "L3_gnn_gamma_p", "L3_gnn_beta_p", "L3_gnn_mean_p",
          "L3_gnn_var_p", "L3_gnn_W_upd", "L3_gnn_b_upd", "L3_gnn_gamma_u", "L3_gnn_beta_u", "L3_gnn_mean_u",
          "L3_gnn_var_u"]


def kernel(**inputs):
    import numpy as np
    import concourse.bacc as bacc
    from concourse import mybir as my
    from concourse.bass_utils import run_bass_kernel_spmd

    nc = bacc.Bacc("TRN2", target_bir_lowering=False, num_devices=1)
    arrays, io = {}, {}
    for name in INPUTS:
        a = np.ascontiguousarray(inputs[name])
        if name == "L1_gnn_epsilon":
            a = a.reshape(1, 1)
        arrays[f"in_{name}"] = a
        io[name] = nc.dram_tensor(f"in_{name}", a.shape, my.dt.from_np(a.dtype), kind="ExternalInput").ap()
    shape = inputs["x"].shape
    io["out"] = nc.dram_tensor("out_x", shape, my.dt.float32, kind="ExternalOutput").ap()
    rows = shape[0] + SPARE
    acc = [nc.dram_tensor(f"acc{j}", (rows, shape[1]), my.dt.float32, kind="Internal").ap() for j in range(4)]
    table = [nc.dram_tensor(f"table{L}", shape, my.dt.float32, kind="Internal").ap() for L in range(4)]
    gnn_layers(nc, io, table, acc)
    r = run_bass_kernel_spmd(nc, [arrays], core_ids=[0])
    return r.results[0]["out_x"]
```
